# Optimizing a Trainium2 kernel written in Bass

```python
import numpy as np
import jax
import jax.numpy as jnp

def _softmax(x, axis=-1):
    return jax.nn.softmax(x, axis=axis)

def _gelu(x):
    return jax.nn.gelu(x, approximate=True)

def _silu(x):
    return jax.nn.silu(x)

def _sigmoid(x):
    return jax.nn.sigmoid(x)

def _layernorm(x, axis=-1, eps=1e-05):
    m = jnp.mean(x, axis=axis, keepdims=True)
    v = jnp.var(x, axis=axis, keepdims=True)
    return (x - m) / jnp.sqrt(v + eps)

def _scatter_add(tgt, idx, src, axis=0):
    return tgt.at[idx].add(src)

def _segment_sum(src, seg, n):
    return jax.ops.segment_sum(src, seg, n)
kernel_name = 'mk_dlrm_tower_d1_rec_r8_28813f'

def setup_inputs(seed: int=0):
    np.random.seed(seed)
    _w = jnp.asarray

    def _rec_inputs():
        import jax
        import jax.numpy as jnp
        _tk = jax.random.key(seed)
        dense_ctx = jax.random.normal(jax.random.fold_in(_tk, 190), (512, 16), jnp.float32)
        ids = jnp.stack([jax.random.randint(jax.random.fold_in(_tk, 200 + f), (512,), 0, v, jnp.int32) for f, v in enumerate([125000, 1250, 12500, 12500, 12500, 12500, 1250, 1250, 125000, 1000, 1250, 1250, 1000, 125000, 125000, 125000, 1250, 1250, 125000, 125000, 1250, 12500, 1000, 12500, 12500, 1250, 1000, 1000, 1000, 1250, 1000, 1000])], axis=1)
        tbl_0 = 0.05 * jax.random.normal(jax.random.fold_in(_tk, 500 + 0), (125000, 32), jnp.float32)
        tbl_1 = 0.05 * jax.random.normal(jax.random.fold_in(_tk, 500 + 1), (1250, 32), jnp.float32)
        tbl_2 = 0.05 * jax.random.normal(jax.random.fold_in(_tk, 500 + 2), (12500, 32), jnp.float32)
        tbl_3 = 0.05 * jax.random.normal(jax.random.fold_in(_tk, 500 + 3), (12500, 32), jnp.float32)
        tbl_4 = 0.05 * jax.random.normal(jax.random.fold_in(_tk, 500 + 4), (12500, 32), jnp.float32)
        tbl_5 = 0.05 * jax.random.normal(jax.random.fold_in(_tk, 500 + 5), (12500, 32), jnp.float32)
        tbl_6 = 0.05 * jax.random.normal(jax.random.fold_in(_tk, 500 + 6), (1250, 32), jnp.float32)
        tbl_7 = 0.05 * jax.random.normal(jax.random.fold_in(_tk, 500 + 7), (1250, 32), jnp.float32)
        tbl_8 = 0.05 * jax.random.normal(jax.random.fold_in(_tk, 500 + 8), (125000, 32), jnp.float32)
        tbl_9 = 0.05 * jax.random.normal(jax.random.fold_in(_tk, 500 + 9), (1000, 32), jnp.float32)
        tbl_10 = 0.05 * jax.random.normal(jax.random.fold_in(_tk, 500 + 10), (1250, 32), jnp.float32)
        tbl_11 = 0.05 * jax.random.normal(jax.random.fold_in(_tk, 500 + 11), (1250, 32), jnp.float32)
        tbl_12 = 0.05 * jax.random.normal(jax.random.fold_in(_tk, 500 + 12), (1000, 32), jnp.float32)
        tbl_13 = 0.05 * jax.random.normal(jax.random.fold_in(_tk, 500 + 13), (125000, 32), jnp.float32)
        tbl_14 = 0.05 * jax.random.normal(jax.random.fold_in(_tk, 500 + 14), (125000, 32), jnp.float32)
        tbl_15 = 0.05 * jax.random.normal(jax.random.fold_in(_tk, 500 + 15), (125000, 32), jnp.float32)
        tbl_16 = 0.05 * jax.random.normal(jax.random.fold_in(_tk, 500 + 16), (1250, 32), jnp.float32)
        tbl_17 = 0.05 * jax.random.normal(jax.random.fold_in(_tk, 500 + 17), (1250, 32), jnp.float32)
        tbl_18 = 0.05 * jax.random.normal(jax.random.fold_in(_tk, 500 + 18), (125000, 32), jnp.float32)
        tbl_19 = 0.05 * jax.random.normal(jax.random.fold_in(_tk, 500 + 19), (125000, 32), jnp.float32)
        tbl_20 = 0.05 * jax.random.normal(jax.random.fold_in(_tk, 500 + 20), (1250, 32), jnp.float32)
        tbl_21 = 0.05 * jax.random.normal(jax.random.fold_in(_tk, 500 + 21), (12500, 32), jnp.float32)
        tbl_22 = 0.05 * jax.random.normal(jax.random.fold_in(_tk, 500 + 22), (1000, 32), jnp.float32)
        tbl_23 = 0.05 * jax.random.normal(jax.random.fold_in(_tk, 500 + 23), (12500, 32), jnp.float32)
        tbl_24 = 0.05 * jax.random.normal(jax.random.fold_in(_tk, 500 + 24), (12500, 32), jnp.float32)
        tbl_25 = 0.05 * jax.random.normal(jax.random.fold_in(_tk, 500 + 25), (1250, 32), jnp.float32)
        tbl_26 = 0.05 * jax.random.normal(jax.random.fold_in(_tk, 500 + 26), (1000, 32), jnp.float32)
        tbl_27 = 0.05 * jax.random.normal(jax.random.fold_in(_tk, 500 + 27), (1000, 32), jnp.float32)
        tbl_28 = 0.05 * jax.random.normal(jax.random.fold_in(_tk, 500 + 28), (1000, 32), jnp.float32)
        tbl_29 = 0.05 * jax.random.normal(jax.random.fold_in(_tk, 500 + 29), (1250, 32), jnp.float32)
        tbl_30 = 0.05 * jax.random.normal(jax.random.fold_in(_tk, 500 + 30), (1000, 32), jnp.float32)
        tbl_31 = 0.05 * jax.random.normal(jax.random.fold_in(_tk, 500 + 31), (1000, 32), jnp.float32)
        _rk = jax.random.fold_in(_tk, 7)
        W_top1 = 0.0606339 * jax.random.normal(jax.random.fold_in(_tk, 801), (272, 512), jnp.float32)
        W_top2 = 0.0441942 * jax.random.normal(jax.random.fold_in(_tk, 802), (512, 256), jnp.float32)
        W_top3 = 0.0625 * jax.random.normal(jax.random.fold_in(_tk, 803), (256, 1), jnp.float32)
        b_top1 = jnp.zeros((512,), jnp.float32)
        b_top2 = jnp.zeros((256,), jnp.float32)
        return (dense_ctx, ids, tbl_0, tbl_1, tbl_2, tbl_3, tbl_4, tbl_5, tbl_6, tbl_7, tbl_8, tbl_9, tbl_10, tbl_11, tbl_12, tbl_13, tbl_14, tbl_15, tbl_16, tbl_17, tbl_18, tbl_19, tbl_20, tbl_21, tbl_22, tbl_23, tbl_24, tbl_25, tbl_26, tbl_27, tbl_28, tbl_29, tbl_30, tbl_31, W_top1, b_top1, W_top2, b_top2, W_top3)
    dense_ctx, ids, tbl_0, tbl_1, tbl_2, tbl_3, tbl_4, tbl_5, tbl_6, tbl_7, tbl_8, tbl_9, tbl_10, tbl_11, tbl_12, tbl_13, tbl_14, tbl_15, tbl_16, tbl_17, tbl_18, tbl_19, tbl_20, tbl_21, tbl_22, tbl_23, tbl_24, tbl_25, tbl_26, tbl_27, tbl_28, tbl_29, tbl_30, tbl_31, W_top1, b_top1, W_top2, b_top2, W_top3 = _rec_inputs()

    def _L0_rec_setup():
        import jax, jax.numpy as jnp
        import numpy as np
        B, F, D = (512, 32, 32)
        LAYER_SIZE = [128, 128]

        def _cin_forward(inputs, filters):
            x0 = inputs
            prev = inputs
            outs = []
            for W in filters:
                z = jnp.einsum('bhd,bmd->bhmd', x0, prev)
                b, h, m, d = z.shape
                z = z.reshape(b, h * m, d)
                cur = jnp.einsum('bpd,pn->bnd', z, W[0])
                cur = jax.nn.relu(cur)
                prev = cur
                outs.append(cur)
            result = jnp.concatenate(outs, axis=1)
            return jnp.sum(result, axis=-1)
        key = jax.random.key(seed)
        k1, k2, k3 = jax.random.split(key, 3)
        inputs = jax.random.normal(k1, (B, F, D), dtype=jnp.float32)
        field_nums = [F] + LAYER_SIZE
        filter_0 = jax.random.normal(k2, (1, field_nums[0] * field_nums[0], field_nums[1]), dtype=jnp.float32) * 0.05
        filter_1 = jax.random.normal(k3, (1, field_nums[0] * field_nums[1], field_nums[2]), dtype=jnp.float32) * 0.05
        return {'inputs': inputs, 'filter_0': filter_0, 'filter_1': filter_1}
    _L0_rec_all = _L0_rec_setup()
    _L0_rec_in = {k: v for k, v in _L0_rec_all.items() if k in ('filter_0', 'filter_1')}
    del _L0_rec_all
    return {'dense_ctx': dense_ctx, 'ids': ids, 'tbl_0': tbl_0, 'tbl_1': tbl_1, 'tbl_2': tbl_2, 'tbl_3': tbl_3, 'tbl_4': tbl_4, 'tbl_5': tbl_5, 'tbl_6': tbl_6, 'tbl_7': tbl_7, 'tbl_8': tbl_8, 'tbl_9': tbl_9, 'tbl_10': tbl_10, 'tbl_11': tbl_11, 'tbl_12': tbl_12, 'tbl_13': tbl_13, 'tbl_14': tbl_14, 'tbl_15': tbl_15, 'tbl_16': tbl_16, 'tbl_17': tbl_17, 'tbl_18': tbl_18, 'tbl_19': tbl_19, 'tbl_20': tbl_20, 'tbl_21': tbl_21, 'tbl_22': tbl_22, 'tbl_23': tbl_23, 'tbl_24': tbl_24, 'tbl_25': tbl_25, 'tbl_26': tbl_26, 'tbl_27': tbl_27, 'tbl_28': tbl_28, 'tbl_29': tbl_29, 'tbl_30': tbl_30, 'tbl_31': tbl_31, 'W_top1': W_top1, 'b_top1': b_top1, 'W_top2': W_top2, 'b_top2': b_top2, 'W_top3': W_top3, 'L0_rec_filter_0': _L0_rec_in['filter_0'], 'L0_rec_filter_1': _L0_rec_in['filter_1']}

def reference(dense_ctx, ids, tbl_0, tbl_1, tbl_2, tbl_3, tbl_4, tbl_5, tbl_6, tbl_7, tbl_8, tbl_9, tbl_10, tbl_11, tbl_12, tbl_13, tbl_14, tbl_15, tbl_16, tbl_17, tbl_18, tbl_19, tbl_20, tbl_21, tbl_22, tbl_23, tbl_24, tbl_25, tbl_26, tbl_27, tbl_28, tbl_29, tbl_30, tbl_31, W_top1, b_top1, W_top2, b_top2, W_top3, L0_rec_filter_0, L0_rec_filter_1):
    import jax
    import jax.numpy as jnp

    def _L0_rec_ref(inputs, filter_0, filter_1):
        import jax, jax.numpy as jnp
        import numpy as np
        B, F, D = (512, 32, 32)
        LAYER_SIZE = [128, 128]

        def _cin_forward(inputs, filters):
            x0 = inputs
            prev = inputs
            outs = []
            for W in filters:
                z = jnp.einsum('bhd,bmd->bhmd', x0, prev)
                b, h, m, d = z.shape
                z = z.reshape(b, h * m, d)
                cur = jnp.einsum('bpd,pn->bnd', z, W[0])
                cur = jax.nn.relu(cur)
                prev = cur
                outs.append(cur)
            result = jnp.concatenate(outs, axis=1)
            return jnp.sum(result, axis=-1)
        return _cin_forward(inputs, (filter_0, filter_1))
    e = jnp.stack([tbl_0[ids[:, 0]], tbl_1[ids[:, 1]], tbl_2[ids[:, 2]], tbl_3[ids[:, 3]], tbl_4[ids[:, 4]], tbl_5[ids[:, 5]], tbl_6[ids[:, 6]], tbl_7[ids[:, 7]], tbl_8[ids[:, 8]], tbl_9[ids[:, 9]], tbl_10[ids[:, 10]], tbl_11[ids[:, 11]], tbl_12[ids[:, 12]], tbl_13[ids[:, 13]], tbl_14[ids[:, 14]], tbl_15[ids[:, 15]], tbl_16[ids[:, 16]], tbl_17[ids[:, 17]], tbl_18[ids[:, 18]], tbl_19[ids[:, 19]], tbl_20[ids[:, 20]], tbl_21[ids[:, 21]], tbl_22[ids[:, 22]], tbl_23[ids[:, 23]], tbl_24[ids[:, 24]], tbl_25[ids[:, 25]], tbl_26[ids[:, 26]], tbl_27[ids[:, 27]], tbl_28[ids[:, 28]], tbl_29[ids[:, 29]], tbl_30[ids[:, 30]], tbl_31[ids[:, 31]]], axis=1)
    z = _L0_rec_ref(e, L0_rec_filter_0, L0_rec_filter_1)
    z = z.reshape(z.shape[0], -1)
    h = jnp.concatenate([z, dense_ctx], axis=1)
    h = jnp.maximum(h @ W_top1 + b_top1, 0.0)
    h = jnp.maximum(h @ W_top2 + b_top2, 0.0)
    y = h @ W_top3
    return y

_drawn_inputs = setup_inputs


def setup_inputs(seed=0):
    import zlib

    import numpy as np

    out = dict(_drawn_inputs(seed))
    spreads = {'b_top1': (0.0, 0.446), 'b_top2': (0.0, 0.432)}
    factors = {'tbl_0': 5.965,
     'tbl_1': 5.947,
     'tbl_2': 6.225,
     'tbl_3': 6.167,
     'tbl_4': 6.127,
     'tbl_5': 5.935,
     'tbl_6': 6.407,
     'tbl_7': 6.16,
     'tbl_8': 6.054,
     'tbl_9': 6.237,
     'tbl_10': 6.054,
     'tbl_11': 6.005,
     'tbl_12': 5.876,
     'tbl_13': 5.636,
     'tbl_14': 6.067,
     'tbl_15': 6.033,
     'tbl_16': 6.167,
     'tbl_17': 5.793,
     'tbl_18': 5.944,
     'tbl_19': 6.348,
     'tbl_20': 5.824,
     'tbl_21': 5.998,
     'tbl_22': 6.138,
     'tbl_23': 5.684,
     'tbl_24': 6.014,
     'tbl_25': 6.185,
     'tbl_26': 5.808,
     'tbl_27': 6.257,
     'tbl_28': 6.252,
     'tbl_29': 6.417,
     'tbl_30': 6.376,
     'tbl_31': 6.322,
     'L0_rec_filter_1': 8.0}
    for name, (base, spread) in spreads.items():
        noise = np.random.default_rng([zlib.crc32(name.encode()), seed]).standard_normal(out[name].shape)
        drawn = base * np.exp(spread * noise) if base else spread * noise
        out[name] = jnp.asarray(drawn.astype(out[name].dtype))
    for name, factor in factors.items():
        out[name] = (out[name] * factor).astype(out[name].dtype)
    return out
```

```python
from contextlib import ExitStack

import concourse.bass as bass
from concourse import mybir

FP32 = mybir.dt.float32
FP32R = mybir.dt.float32r
INT32 = mybir.dt.int32
ALU = mybir.AluOpType
ACT = mybir.ActivationFunctionType

B, F, D = 512, 32, 32
N1 = N2 = 128
DENSE, H1, H2 = 16, 512, 256
P = 128
BLOCKS = B // P
DC = 4
COLS = DC * P
CPB = D // DC
CHUNKS = BLOCKS * CPB
HG = COLS // N2
GROUPS = F // HG
EACH = GROUPS // 2
SLOTS = DC * GROUPS
SHIFTS = F // 2
COPIES = P // F
PAIRS = 2
TREE = 4

PE_X4 = 3
PE_SHIFT = {9: 0, 10: 1, 14: 2, 16: 3, 20: 4}
PE_PRODUCT = {15: 1, 18: 0, 20: 2, 23: 3, 26: 4}
PRODUCT_ORDER = [1, 0, 2, 3, 4]
DVE_PAIR = {10: 0, 12: 1, 16: 2, 18: 3, 22: 4}
DVE_XLOW, DVE_LOW16, DVE_LOW = 6, 14, 28
ACT_X0, ACT_X4, ACT_HIGH16, ACT_HIGH = 1, 5, 13, 27
STEPS = 5


def dlrm_tower(nc, ids, tables, w0_ab, w0_ba, w0_half, w1, w_top1, b_top1, w_top2, b_top2, w_top3, dense_t,
               identity, select, out):
    ctx = ExitStack()
    with ctx:
        def sb(name, shape, dt=FP32):
            return ctx.enter_context(nc.sbuf_tensor(name, shape, dt))

        def sem(name):
            return ctx.enter_context(nc.semaphore(name))

        ident = sb("ident", [P, P])
        ids_sb = sb("ids_sb", [P, BLOCKS, F], INT32)
        ids_next = sb("ids_next", [P, F], INT32)
        rows_next = sb("rows_next", [P, F, D])
        rows = sb("rows", [P, BLOCKS, F, D])
        x0 = [sb(f"x0_{i}", [P, DC, P]) for i in range(2)]
        x4 = [sb(f"x4_{i}", [P, COLS]) for i in range(2)]
        x_hl = sb("x_hl", [P, COLS], FP32R)
        select_sb = sb("select_sb", [P, STEPS, P])
        select_r = sb("select_r", [P, STEPS, P], FP32R)
        pair = [sb(f"pair_{i}", [P, COLS]) for i in range(2)]
        pair16 = sb("pair16", [P, COLS])
        pair16_hl = sb("pair16_hl", [P, COLS], FP32R)
        w0_sb = sb("w0_sb", [P, STEPS - 1, N1])
        w0_t = sb("w0_t", [P, STEPS - 1, N1])
        w0_half_sb = sb("w0_half_sb", [P, N1])
        w0_half_hl = sb("w0_half_hl", [P, N1], FP32R)
        w1_sb = sb("w1_sb", [P, F, N2])
        w1_high = sb("w1_high", [P, F * N2], FP32R)
        w1_low = sb("w1_low", [P, F * N2], FP32R)
        cur_high = [sb(f"cur_high_{i}", [P, COLS], FP32R) for i in range(2)]
        cur_low = [sb(f"cur_low_{i}", [P, COLS], FP32R) for i in range(2)]
        sum1 = sb("sum1", [P, BLOCKS, DC, P])
        acc = [sb(f"acc_{i}", [P, 2, N2]) for i in range(4)]
        prod = [sb(f"prod_{i}", [P, EACH * HG * N2]) for i in range(2)]
        half = sb("half", [P, 1024 + 512 + 256])
        act_sum = [sb(f"act_sum_{i}", [P, N2]) for i in range(4)]
        dve_sum = sb("dve_sum", [P, N2])
        tile_sum = sb("tile_sum", [P, N2])
        sum2 = sb("sum2", [P, BLOCKS, N2])
        wt1 = sb("wt1", [P, 2, H1])
        wt1_dense = sb("wt1_dense", [DENSE, H1])
        wt2 = sb("wt2", [P, H1 // P, H2])
        wt3 = sb("wt3", [P, H2 // P])
        bt1 = sb("bt1", [P, H1 // P])
        bt2 = sb("bt2", [P, H2 // P])
        dense_sb = sb("dense_sb", [DENSE, B])
        z1 = sb("z1", [P, B])
        z1_half = sb("z1_half", [P, BLOCKS, 2, P])
        z2 = sb("z2", [P, B])
        a1 = sb("a1", [P, H1 // P, B])
        a2 = sb("a2", [P, H2 // P, B])
        y_sb = sb("y_sb", [1, B])

        bank = [ctx.enter_context(nc.psum_tensor(f"bank{i}", [P, COLS], FP32)) for i in range(8)]
        dve_bank, act_bank, shift_bank, cur_bank, x4_bank = bank[0:2], bank[2:4], bank[4:6], bank[6], bank[7]

        ids_in = sem("ids_in")
        w1_in = sem("w1_in")
        w0_in = sem("w0_in")
        top_in = sem("top_in")
        zeroed = sem("zeroed")
        w1_high_done = sem("w1_high_done")
        w1_low_done = sem("w1_low_done")
        w0_done = sem("w0_done")
        w0_half_high = sem("w0_half_high")
        gathered = sem("gathered")
        ids_moved = sem("ids_moved")
        rows_ready = sem("rows_ready")
        x0_ready = sem("x0_ready")
        select_done = sem("select_done")
        transposed = sem("transposed")
        shifted = sem("shifted")
        x4_ready = sem("x4_ready")
        x_low = sem("x_low")
        paired = sem("paired")
        high16 = sem("high16")
        low16 = sem("low16")
        multiplied = sem("multiplied")
        cur_high_ready = sem("cur_high_ready")
        cur_low_ready = sem("cur_low_ready")
        for_dve = sem("for_dve")
        for_act = sem("for_act")
        mac = sem("mac")
        act_prod = sem("act_prod")
        tree = sem("tree")
        folded = sem("folded")
        z1_step = sem("z1_step")
        z2_turned = sem("z2_turned")
        z2_ready = sem("z2_ready")
        top_product = sem("top_product")
        top_relu = sem("top_relu")
        y_ready = sem("y_ready")
        y_out = sem("y_out")

        block = ctx.enter_context(nc.Block())
        MACS = HG * EACH

        def wait(eng, semaphore, value):
            if not isinstance(value, int) or value > 0:
                eng.wait_ge(semaphore, value)

        def block_of(chunk):
            if isinstance(chunk, int):
                return chunk // CPB
            return (chunk >> (CPB.bit_length() - 1)).with_bounds(min_val=0, max_val=BLOCKS - 1)

        def in_block(chunk):
            if isinstance(chunk, int):
                return chunk % CPB
            return (chunk & (CPB - 1)).with_bounds(min_val=0, max_val=CPB - 1)

        def body_loop(eng, body):
            body(0, True, False)
            with eng.Fori(1, CHUNKS // PAIRS - 1) as pair_no:
                body(pair_no * PAIRS, False, False)
            body(CHUNKS - PAIRS, False, True)

        @block.sync
        def _(sp):
            sp.dma_start(ids_sb[:], ids.rearrange("(k p) f -> p k f", p=P)).then_inc(ids_in, 16)
            sp.dma_start(ident[:], identity).then_inc(w0_in, 16)
            sp.dma_start(w0_sb[:], w0_ab).then_inc(w0_in, 16)
            sp.dma_start(w0_t[:], w0_ba).then_inc(w0_in, 16)
            sp.dma_start(w0_half_sb[:], w0_half).then_inc(w0_in, 16)
            sp.dma_start(select_sb[:], select).then_inc(w0_in, 16)
            sp.dma_start(w1_sb[:], w1.rearrange("(h m) n -> m h n", h=F)).then_inc(w1_in, 16)
            sp.dma_start(wt1[:], w_top1[0:2 * P, :].rearrange("(k p) n -> p k n", p=P)).then_inc(top_in, 16)
            sp.dma_start(wt1_dense[:], w_top1[2 * P:, :]).then_inc(top_in, 16)
            sp.dma_start(wt2[:], w_top2.rearrange("(k p) n -> p k n", p=P)).then_inc(top_in, 16)
            sp.dma_start(wt3[:], w_top3).then_inc(top_in, 16)
            sp.dma_start(bt1[:], b_top1).then_inc(top_in, 16)
            sp.dma_start(bt2[:], b_top2).then_inc(top_in, 16)
            sp.dma_start(dense_sb[:], dense_t).then_inc(top_in, 16)
            sp.wait_ge(y_ready, 1)
            sp.dma_start(out.rearrange("b o -> o b"), y_sb[:]).then_inc(y_out, 16)
            sp.wait_ge(y_out, 16)

        @block.gpsimd
        def _(pool):
            pool.wait_ge(ids_in, 16)
            for f in range(F):
                nc.gpsimd.indirect_dma_start(
                    out=rows[:, 0, f, :], out_offset=None, in_=tables[f],
                    in_offset=bass.IndirectOffsetOnAxis(ids_sb[:, 0, f:f + 1], 0)).then_inc(gathered, 16)

            def sum_products(tile, t):
                src, width, at = prod[t % 2], EACH * HG * N2 // 2, 0
                pool.wait_ge(act_prod, (tile + 1) * EACH)
                for level in range(TREE):
                    if level > 0:
                        pool.wait_ge(tree, tile * TREE + level)
                    if level == TREE - 1:
                        dst = act_sum[t % 4][:]
                        wait(pool, folded, (tile - 4) * 3 + 2)
                    else:
                        dst = half[:, at:at + width]
                    nc.gpsimd.tensor_tensor(dst, src[:, 0:width], src[:, width:2 * width],
                                            ALU.add).then_inc(tree, 1)
                    src, at, width = dst, at + width, width // 2

            tiles = CPB * DC
            spots = {t * (tiles - 8) // F: [] for t in range(F)}
            for f in range(F):
                spots[f * (tiles - 8) // F].append(f)

            def block_body(k, more):
                if more:
                    pool.wait_ge(gathered, (k + 1) * F * 16)
                    nc.gpsimd.tensor_copy(ids_next[:], ids_sb[:, bass.ds(k + 1, 1), :].rearrange(
                        "p o f -> p (o f)")).then_inc(ids_moved, 1)
                    pool.wait_ge(ids_moved, k + 1)
                    pool.wait_ge(rows_ready, k + 1)
                for t in range(tiles):
                    sum_products(k * tiles + t, t)
                    for f in spots.get(t, []) if more else []:
                        nc.gpsimd.indirect_dma_start(
                            out=rows_next[:, f, :], out_offset=None, in_=tables[f],
                            in_offset=bass.IndirectOffsetOnAxis(ids_next[:, f:f + 1], 0)).then_inc(gathered, 16)
                    if more and t == tiles - 7:
                        pool.wait_ge(gathered, (k + 2) * F * 16)
                        nc.gpsimd.tensor_copy(
                            rows[:, bass.ds(k + 1, 1), :, :].rearrange("p o f d -> p (o f d)"),
                            rows_next[:].rearrange("p f d -> p (f d)")).then_inc(rows_ready, 1)

            pool.wait_ge(gathered, F * 16)
            nc.gpsimd.memset(half[:, 0:1], 0.0).then_inc(rows_ready, 1)
            block_body(0, True)
            with pool.Fori(1, BLOCKS - 1) as k:
                block_body(k, True)
            block_body(BLOCKS - 1, False)

        def act_x0(act, c, u):
            act.wait_ge(rows_ready, block_of(c) + 1)
            wait(act, act_prod, (c - 1) * (EACH * DC))
            wait(act, mac, (c - 1) * (MACS * DC))
            wait(act, transposed, c - 1)
            src = rows[:, bass.ds(block_of(c), 1), :, bass.ds(in_block(c) * DC, DC)].rearrange("p o f d -> p d (o f)")
            nc.scalar.copy(x0[u][:].rearrange("p d (k f) -> p d k f", k=COPIES),
                           src.unsqueeze(2).to_broadcast([P, DC, COPIES, F])).then_inc(x0_ready, 1)

        def act_x4(act, c, u):
            act.wait_ge(transposed, c + 1)
            wait(act, paired, (c - 1) * STEPS)
            nc.scalar.copy(x4[u][:], x4_bank[:]).then_inc(x4_ready, 1)
            wait(act, shifted, c * STEPS)
            nc.scalar.copy(x_hl[:], x4_bank[:]).then_inc(x4_ready, 1)

        def act_high16(act, c):
            act.wait_ge(paired, c * STEPS + 1)
            wait(act, multiplied, (c - 1) * STEPS + 2)
            nc.scalar.copy(pair16_hl[:], pair16[:]).then_inc(high16, 1)

        def act_high(act, c, u):
            act.wait_ge(multiplied, (c + 1) * STEPS)
            wait(act, for_act, (c - 1) * (EACH * DC))
            nc.scalar.activation(cur_high[u][:], cur_bank[:], ACT.Relu).then_inc(cur_high_ready, 1)

        @block.scalar
        def _(act):
            act.wait_ge(w0_in, 80)
            nc.scalar.copy(w0_half_hl[:], w0_half_sb[:]).then_inc(w0_half_high, 1)
            act.wait_ge(w1_in, 16)
            nc.scalar.copy(w1_high[:], w1_sb[:].rearrange("m h n -> m (h n)")).then_inc(w1_high_done, 1)
            act_x0(act, 0, 0)
            act_x4(act, 0, 0)
            act_high16(act, 0)
            act_high(act, 0, 0)

            def body(first_chunk, first, last):
                for u in range(PAIRS):
                    c = first_chunk + u
                    for t in range(DC):
                        tile = c * DC + t
                        wait(act, tree, (tile - 2) * TREE + 1)
                        for e in range(EACH):
                            act.wait_ge(for_act, tile * EACH + e + 1)
                            for i in range(HG):
                                h = (2 * e + 1) * HG + i
                                at = (e * HG + i) * N2
                                ins = nc.scalar.activation(
                                    prod[t % 2][:, at:at + N2], act_bank[e % 2][:, i * N2:(i + 1) * N2],
                                    ACT.Copy, scale=x0[u][:, t, h:h + 1])
                            ins.then_inc(act_prod, 1)
                            slot = t * GROUPS + 2 * e + 1
                            if last and u == PAIRS - 1:
                                continue
                            if slot == ACT_X0:
                                act_x0(act, c + 1, 1 - u)
                            if slot == ACT_X4:
                                act_x4(act, c + 1, 1 - u)
                            if slot == ACT_HIGH16:
                                act_high16(act, c + 1)
                            if slot == ACT_HIGH:
                                act_high(act, c + 1, 1 - u)

            body_loop(act, body)

            act.wait_ge(z2_turned, 1)
            nc.scalar.copy(z2[:], bank[0][:]).then_inc(z2_ready, 1)
            act.wait_ge(top_in, 7 * 16)
            for i in range(H1 // P):
                act.wait_ge(top_product, i + 1)
                nc.scalar.activation(a1[:, i, :], bank[1 + i][:], ACT.Relu,
                                     bias=bt1[:, i:i + 1]).then_inc(top_relu, 1)
            for i in range(H2 // P):
                act.wait_ge(top_product, H1 // P + i + 1)
                nc.scalar.activation(a2[:, i, :], bank[5 + i][:], ACT.Relu,
                                     bias=bt2[:, i:i + 1]).then_inc(top_relu, 1)
            act.wait_ge(top_product, H1 // P + H2 // P + 1)
            nc.scalar.copy(y_sb[:], bank[7][0:1, :]).then_inc(y_ready, 1)

        def dve_xlow(dve, c, u):
            dve.wait_ge(x4_ready, (c + 1) * 2)
            nc.vector.tensor_tensor(x_hl[P // 2:, :], x4[u][P // 2:, :], x_hl[P // 2:, :].bitcast(FP32),
                                    ALU.subtract).then_inc(x_low, 1)

        def dve_pair(dve, c, u, step):
            dve.wait_ge(shifted, c * STEPS + step + 1)
            if step == 0:
                wait(dve, low16, c)
                wait(dve, high16, c)
                dst = pair16
            else:
                wait(dve, multiplied, {1: (c - 1) * STEPS + 4, 2: c * STEPS, 3: c * STEPS + 1,
                                       4: c * STEPS + 3}[step])
                dst = pair[step % 2]
            nc.vector.tensor_tensor(dst[:], shift_bank[step % 2][:], x4[u][:], ALU.mult).then_inc(paired, 1)

        def dve_low16(dve, c):
            dve.wait_ge(high16, c + 1)
            nc.vector.tensor_tensor(pair16_hl[P // 2:, :], pair16[P // 2:, :], pair16_hl[P // 2:, :].bitcast(FP32),
                                    ALU.subtract).then_inc(low16, 1)

        def dve_low(dve, c, u, k):
            dve.wait_ge(cur_high_ready, c + 1)
            wait(dve, for_act, (c - 1) * (EACH * DC))
            nc.vector.scalar_tensor_tensor(
                out=cur_low[u][:], in0=cur_bank[:], scalar=0.0, in1=cur_high[u][:].bitcast(FP32),
                op0=ALU.max, op1=ALU.subtract).then_inc(cur_low_ready, 1)
            s1 = sum1[:, bass.ds(k, 1), :, :].rearrange("p o d b -> p (o d b)")
            wait(dve, cur_low_ready, c * 2)
            nc.vector.scalar_tensor_tensor(
                out=s1, in0=cur_bank[:], scalar=0.0, in1=s1, op0=ALU.max, op1=ALU.add).then_inc(cur_low_ready, 1)

        def dve_fold(dve, tile, t, k, step):
            if step == 0:
                wait(dve, mac, (tile + 1) * MACS)
                nc.vector.tensor_tensor(dve_sum[:], acc[t % 4][:, 0, :], acc[t % 4][:, 1, :],
                                        ALU.add).then_inc(folded, 1)
            if step == 1:
                dve.wait_ge(tree, (tile + 1) * TREE)
                dve.wait_ge(folded, tile * 3 + 1)
                nc.vector.tensor_tensor(tile_sum[:], dve_sum[:], act_sum[t % 4][:], ALU.add).then_inc(folded, 1)
            if step == 2:
                dve.wait_ge(folded, tile * 3 + 2)
                s2 = sum2[:, bass.ds(k, 1), :].rearrange("p o n -> p (o n)")
                nc.vector.scalar_tensor_tensor(
                    out=s2, in0=tile_sum[:], scalar=0.0, in1=s2, op0=ALU.max, op1=ALU.add).then_inc(folded, 1)

        @block.vector
        def _(dve):
            nc.vector.memset(sum1[:], 0.0).then_inc(zeroed, 1)
            nc.vector.memset(sum2[:], 0.0).then_inc(zeroed, 1)
            dve.wait_ge(w0_in, 80)
            nc.vector.tensor_copy(select_r[:], select_sb[:]).then_inc(select_done, 1)
            for lo, hi, j in ((F, 2 * F, 0), (2 * F, P, 0), (0, P, 1)):
                js = slice(j, STEPS - 1) if j else slice(0, 1)
                last = nc.vector.tensor_tensor(w0_sb[lo:hi, js, :], w0_sb[lo:hi, js, :], w0_t[lo:hi, js, :], ALU.add)
            last.then_inc(w0_done, 1)
            dve.wait_ge(w0_half_high, 1)
            for q in (1, 3):
                rows32 = slice(q * F, (q + 1) * F)
                last = nc.vector.tensor_tensor(w0_half_hl[rows32, :], w0_half_sb[rows32, :],
                                               w0_half_hl[rows32, :].bitcast(FP32), ALU.subtract)
            last.then_inc(w0_done, 1)
            dve.wait_ge(w1_high_done, 1)
            nc.vector.tensor_tensor(w1_low[:], w1_sb[:].rearrange("m h n -> m (h n)"), w1_high[:].bitcast(FP32),
                                    ALU.subtract).then_inc(w1_low_done, 1)
            dve.wait_ge(zeroed, 2)
            dve_xlow(dve, 0, 0)
            for step in range(STEPS):
                dve_pair(dve, 0, 0, step)
                if step == 1:
                    dve_low16(dve, 0)
            dve_low(dve, 0, 0, 0)

            def body(first_chunk, first, last):
                for u in range(PAIRS):
                    c = first_chunk + u
                    for t in range(DC):
                        tile = c * DC + t
                        old, old_t = tile - 2, u * DC + t - 2
                        old_block = block_of(first_chunk if old_t >= 0 else first_chunk - PAIRS)
                        for e in range(EACH):
                            dve.wait_ge(for_dve, tile * EACH + e + 1)
                            for i in range(HG):
                                n, h = e * HG + i, 2 * e * HG + i
                                scalar = x0[u][:, t, h:h + 1]
                                src = dve_bank[e % 2][:, i * N2:(i + 1) * N2]
                                dst = acc[t % 4][:, n % 2, :]
                                if n < 2:
                                    nc.vector.tensor_scalar(dst, src, scalar, None, ALU.mult).then_inc(mac, 1)
                                    continue
                                dve.wait_ge(mac, tile * MACS + n - 1)
                                nc.vector.scalar_tensor_tensor(
                                    out=dst, in0=src, scalar=scalar, in1=dst, op0=ALU.mult,
                                    op1=ALU.add).then_inc(mac, 1)
                            if e < 3 and not (first and old_t < 0):
                                dve_fold(dve, old, old_t, old_block, e)
                            slot = t * GROUPS + 2 * e
                            if last and u == PAIRS - 1:
                                continue
                            if slot == DVE_XLOW:
                                dve_xlow(dve, c + 1, 1 - u)
                            if slot in DVE_PAIR:
                                dve_pair(dve, c + 1, 1 - u, DVE_PAIR[slot])
                            if slot == DVE_LOW16:
                                dve_low16(dve, c + 1)
                            if slot == DVE_LOW:
                                dve_low(dve, c + 1, 1 - u, block_of(c + 1))

            body_loop(dve, body)
            for tile in (CHUNKS * DC - 2, CHUNKS * DC - 1):
                for step in range(3):
                    dve_fold(dve, tile, tile, BLOCKS - 1, step)
            dve.wait_ge(cur_low_ready, CHUNKS * 2)
            nc.vector.tensor_tensor(z1_half[:], sum1[:, :, 0:2, :], sum1[:, :, 2:4, :], ALU.add).then_inc(z1_step, 1)
            dve.wait_ge(z1_step, 1)
            nc.vector.tensor_tensor(z1[:].rearrange("p (k b) -> p k b", k=BLOCKS), z1_half[:, :, 0, :],
                                    z1_half[:, :, 1, :], ALU.add).then_inc(z1_step, 1)

        def pe_x4(pe, c, u):
            pe.wait_ge(x0_ready, c + 1)
            wait(pe, x4_ready, c * 2)
            for d in range(DC):
                last = nc.tensor.transpose(x4_bank[:, d * P:(d + 1) * P], x0[u][:, d, :], ident[:])
            last.then_inc(transposed, 1)

        def pe_shift(pe, c, step):
            pe.wait_ge(x_low, c + 1)
            wait(pe, paired, {0: c * STEPS, 1: (c - 1) * STEPS + 4}.get(step, c * STEPS + step - 1))
            nc.tensor.matmul(shift_bank[step % 2][:], select_r[:, step, :], x_hl[:], start=True,
                             stop=True).then_inc(shifted, 1)

        def pe_product(pe, c, step):
            if step == PRODUCT_ORDER[0]:
                wait(pe, cur_low_ready, c * 2)
            if step == 0:
                pe.wait_ge(low16, c + 1)
                ins = nc.tensor.matmul(cur_bank[:], w0_half_hl[:], pair16_hl[:], start=False, stop=False)
            else:
                pe.wait_ge(paired, c * STEPS + step + 1)
                ins = nc.tensor.matmul(cur_bank[:], w0_sb[:, step - 1, :], pair[step % 2][:],
                                       start=step == PRODUCT_ORDER[0], stop=step == PRODUCT_ORDER[-1])
            ins.then_inc(multiplied, 1)

        @block.tensor
        def _(pe):
            pe.wait_ge(w0_in, 80)
            pe_x4(pe, 0, 0)
            pe.wait_ge(select_done, 1)
            pe_shift(pe, 0, 0)
            pe_shift(pe, 0, 1)
            pe.wait_ge(w0_done, 2)
            for step in range(2, STEPS):
                pe_shift(pe, 0, step)
                for done in {2: [1, 0], 3: [2], 4: [3]}[step]:
                    pe_product(pe, 0, done)
            pe_product(pe, 0, 4)
            pe.wait_ge(w1_low_done, 1)

            def body(first_chunk, first, last):
                for u in range(PAIRS):
                    c = first_chunk + u
                    for t in range(DC):
                        tile = c * DC + t
                        tile_cols = slice(t * P, (t + 1) * P)
                        for g in range(GROUPS):
                            e = g // 2
                            if g % 2 == 0:
                                dst, ready = dve_bank[e % 2], for_dve
                                wait(pe, mac, (tile * EACH + e - 1) * HG)
                            else:
                                dst, ready = act_bank[e % 2], for_act
                                wait(pe, act_prod, tile * EACH + e - 1)
                            if t == 0 and g == 0:
                                pe.wait_ge(cur_high_ready, c + 1)
                            fields = slice(g * COLS, (g + 1) * COLS)
                            nc.tensor.matmul(dst[:], cur_high[u][:, tile_cols], w1_high[:, fields],
                                             start=True, stop=False)
                            nc.tensor.matmul(dst[:], cur_high[u][:, tile_cols], w1_low[:, fields],
                                             start=False, stop=False)
                            if t == 0 and g == 0:
                                pe.wait_ge(cur_low_ready, c * 2 + 1)
                            nc.tensor.matmul(dst[:], cur_low[u][:, tile_cols], w1_high[:, fields],
                                             start=False, stop=True).then_inc(ready, 1)
                            slot = t * GROUPS + g
                            if last and u == PAIRS - 1:
                                continue
                            if slot == PE_X4:
                                pe_x4(pe, c + 1, 1 - u)
                            if slot in PE_SHIFT:
                                pe_shift(pe, c + 1, PE_SHIFT[slot])
                            if slot in PE_PRODUCT:
                                pe_product(pe, c + 1, PE_PRODUCT[slot])

            body_loop(pe, body)

            pe.wait_ge(folded, CHUNKS * DC * 3)
            for k in range(BLOCKS):
                last = nc.tensor.transpose(bank[0][:, k * P:(k + 1) * P], sum2[:, k, :], ident[:])
            last.then_inc(z2_turned, 1)
            pe.wait_ge(top_in, 7 * 16)
            pe.wait_ge(z1_step, 2)
            pe.wait_ge(act_prod, CHUNKS * DC * EACH)
            for i in range(H1 // P):
                n = slice(i * P, (i + 1) * P)
                nc.tensor.matmul(bank[1 + i][:], wt1[:, 0, n], z1[:], start=True, stop=False)
                nc.tensor.matmul(bank[1 + i][:], wt1_dense[:, n], dense_sb[:], start=False, stop=False)
                if i == 0:
                    pe.wait_ge(z2_ready, 1)
                nc.tensor.matmul(bank[1 + i][:], wt1[:, 1, n], z2[:], start=False, stop=True).then_inc(top_product, 1)
            for i in range(H2 // P):
                for k in range(H1 // P):
                    if i == 0:
                        pe.wait_ge(top_relu, k + 1)
                    ins = nc.tensor.matmul(bank[5 + i][:], wt2[:, k, i * P:(i + 1) * P], a1[:, k, :],
                                           start=k == 0, stop=k == H1 // P - 1)
                ins.then_inc(top_product, 1)
            for k in range(H2 // P):
                pe.wait_ge(top_relu, H1 // P + k + 1)
                ins = nc.tensor.matmul(bank[7][0:1, :], wt3[:, k:k + 1], a2[:, k, :], start=k == 0,
                                       stop=k == H2 // P - 1)
            ins.then_inc(top_product, 1)


def kernel(**inputs):
    import numpy as np
    import concourse.bacc as bacc
    from concourse.bass_utils import run_bass_kernel_spmd

    f0 = np.asarray(inputs["L0_rec_filter_0"]).reshape(F, F, N1)
    h = np.arange(F)
    k = np.arange(SHIFTS)
    partner = (h[None, :] + k[:, None]) % F

    select = np.zeros((P, STEPS, COPIES, F), np.float32)
    for step in range(STEPS):
        for copy in range(COPIES):
            shift = SHIFTS if step == 0 else (step - 1) * COPIES + copy
            for half in (0, P // 2):
                select[half + (h + shift) % F, step, copy, h] = 1

    def shifts(w):
        return np.ascontiguousarray(w.reshape(STEPS - 1, 4, F, N1).transpose(1, 2, 0, 3).reshape(P, STEPS - 1, N1))

    arrays = {
        "ids_dram": np.ascontiguousarray(inputs["ids"]),
        "w0_ab_dram": shifts(f0[np.broadcast_to(h, partner.shape), partner]),
        "w0_ba_dram": shifts(f0[partner, np.broadcast_to(h, partner.shape)]),
        "w0_half_dram": np.tile(f0[h, (h + SHIFTS) % F], (P // F, 1)),
        "w1_dram": np.asarray(inputs["L0_rec_filter_1"]).reshape(F * N1, N2),
        "w_top1_dram": np.asarray(inputs["W_top1"]),
        "b_top1_dram": np.ascontiguousarray(np.asarray(inputs["b_top1"]).reshape(H1 // P, P).T),
        "w_top2_dram": np.asarray(inputs["W_top2"]),
        "b_top2_dram": np.ascontiguousarray(np.asarray(inputs["b_top2"]).reshape(H2 // P, P).T),
        "w_top3_dram": np.ascontiguousarray(np.asarray(inputs["W_top3"]).reshape(H2 // P, P).T),
        "dense_dram": np.ascontiguousarray(np.asarray(inputs["dense_ctx"]).T),
        "identity_dram": np.eye(P, dtype=np.float32),
        "select_dram": select.reshape(P, STEPS, P),
    }
    for f in range(F):
        arrays[f"table_{f}_dram"] = np.asarray(inputs[f"tbl_{f}"])

    nc = bacc.Bacc("TRN2", target_bir_lowering=False, num_devices=1)
    ap = {n: nc.dram_tensor(n, a.shape, mybir.dt.from_np(a.dtype), kind="ExternalInput").ap()
          for n, a in arrays.items()}
    out = nc.dram_tensor("y_dram", (B, 1), FP32, kind="ExternalOutput").ap()
    dlrm_tower(nc, ap["ids_dram"], [ap[f"table_{f}_dram"] for f in range(F)], ap["w0_ab_dram"], ap["w0_ba_dram"],
               ap["w0_half_dram"], ap["w1_dram"], ap["w_top1_dram"], ap["b_top1_dram"], ap["w_top2_dram"],
               ap["b_top2_dram"], ap["w_top3_dram"], ap["dense_dram"], ap["identity_dram"],
               ap["select_dram"], out)
    r = run_bass_kernel_spmd(nc, [arrays], core_ids=[0])
    return r.results[0]["y_dram"]
```

```python
from contextlib import ExitStack

import concourse.bass as bass
from concourse import mybir

FP32 = mybir.dt.float32
FP32R = mybir.dt.float32r
INT32 = mybir.dt.int32
ALU = mybir.AluOpType
ACT = mybir.ActivationFunctionType

B, F, D = 512, 32, 32
N1 = N2 = 128
DENSE, H1, H2 = 16, 512, 256
P = 128
BLOCKS = B // P
DC = 4
COLS = DC * P
CPB = D // DC
CHUNKS = BLOCKS * CPB
HG = COLS // N2
GROUPS = F // HG
EACH = GROUPS // 2
SLOTS = DC * GROUPS
SHIFTS = F // 2
COPIES = P // F
UNROLL = 2
CPAIRS = DC // 2
TREE = 3
TOTALS = 4

DVE_PAIR = {0: 1, 4: 0, 8: 2, 12: 3, 16: 4}
PAIR_ORDER = list(DVE_PAIR.values())
PE_PRODUCT = {8: 1, 14: 2, 18: 3, 20: 0, 22: 4}
PRODUCT_ORDER = list(PE_PRODUCT.values())
ACT_HIGH16, DVE_LOW16 = 9, 12
ACT_HIGH, DVE_LOW, DVE_SUM = 25, 28, 0
ACT_X0 = 17
ACT_TURN, PE_TURN, ACT_TURNED = 4, 8, 13
STEPS = 5


def dlrm_tower(nc, ids, tables, w0_ab, w0_ba, w0_half, w1, w_top1, b_top1, w_top2, b_top2, w_top3, dense_t,
               identity, parity, x0_dram, out):
    ctx = ExitStack()
    with ctx:
        def sb(name, shape, dt=FP32):
            return ctx.enter_context(nc.sbuf_tensor(name, shape, dt))

        def sem(name):
            return ctx.enter_context(nc.semaphore(name))

        ident = sb("ident", [P, P])
        ids_sb = sb("ids_sb", [P, BLOCKS, F], INT32)
        ids_next = sb("ids_next", [P, F], INT32)
        rows_next = sb("rows_next", [P, F, D])
        rows = sb("rows", [P, BLOCKS, F, D])
        x0 = [sb(f"x0_{i}", [P, F, DC]) for i in range(2)]
        turn_in = sb("turn_in", [P, DC * F])
        turned = sb("turned", [P, P])
        x4 = [sb(f"x4_{i}", [P, COLS]) for i in range(2)]
        shifts = [sb(f"shifts_{i}", [P, STEPS, COLS]) for i in range(2)]
        pair = [sb(f"pair_{i}", [P, COLS]) for i in range(3)]
        pair16 = sb("pair16", [P, COLS])
        pair16_hl = sb("pair16_hl", [P, COLS], FP32R)
        w0_sb = sb("w0_sb", [P, STEPS - 1, N1])
        w0_t = sb("w0_t", [P, STEPS - 1, N1])
        w0_half_sb = sb("w0_half_sb", [P, N1])
        w0_half_r = sb("w0_half_r", [P, N1], FP32R)
        w0_half_hl = sb("w0_half_hl", [P, N1], FP32R)
        parity_sb = sb("parity_sb", [P, 2])
        w1_sb = sb("w1_sb", [P, F, N2])
        w1_high = sb("w1_high", [P, F * N2], FP32R)
        w1_low = sb("w1_low", [P, F * N2], FP32R)
        cur_high = [sb(f"cur_high_{i}", [P, COLS], FP32R) for i in range(2)]
        cur_low = [sb(f"cur_low_{i}", [P, COLS], FP32R) for i in range(2)]
        sum1 = sb("sum1", [P, BLOCKS, DC, P])
        acc = sb("acc", [P, 4, 2, N2])
        parts = [[sb(f"parts_{i}{j}", [P, EACH * HG * N2]) for j in range(2)] for i in range(2)]
        half = sb("half", [P, 1024 + 512])
        left = [sb(f"left_{i}", [P, 2, 2, N2]) for i in range(TOTALS)]
        total = sb("total", [P, 2, N2])
        sum2 = sb("sum2", [P, BLOCKS, 2, N2])
        z2_rows = sb("z2_rows", [P, BLOCKS, N2])
        wt1 = sb("wt1", [P, 2, H1])
        wt1_dense = sb("wt1_dense", [DENSE, H1])
        wt2 = sb("wt2", [P, H1 // P, H2])
        wt3 = sb("wt3", [P, H2 // P])
        bt1 = sb("bt1", [P, H1 // P])
        bt2 = sb("bt2", [P, H2 // P])
        dense_sb = sb("dense_sb", [DENSE, B])
        z1 = sb("z1", [P, B])
        z1_half = sb("z1_half", [P, BLOCKS, 2, P])
        z2 = sb("z2", [P, B])
        free = w1_sb[:].rearrange("p h n -> p (h n)")
        a1 = free[:, 0:H1 // P * B].rearrange("p (k b) -> p k b", b=B)
        a2 = free[:, H1 // P * B:(H1 + H2) // P * B].rearrange("p (k b) -> p k b", b=B)
        y_sb = sb("y_sb", [1, B])

        bank = [ctx.enter_context(nc.psum_tensor(f"bank{i}", [P, COLS], FP32)) for i in range(8)]
        dve_bank, act_bank, cur_bank, turn_bank = bank[0:4], bank[4:6], bank[6], bank[7]

        ids_in = sem("ids_in")
        w1_in = sem("w1_in")
        w0_in = sem("w0_in")
        top_in = sem("top_in")
        zeroed = sem("zeroed")
        w1_high_done = sem("w1_high_done")
        w1_low_done = sem("w1_low_done")
        w0_done = sem("w0_done")
        w0_half_high = sem("w0_half_high")
        gathered = sem("gathered")
        ids_moved = sem("ids_moved")
        rows_ready = sem("rows_ready")
        x0_ready = sem("x0_ready")
        turn_ready = sem("turn_ready")
        transposed = sem("transposed")
        turned_ready = sem("turned_ready")
        written = sem("written")
        loaded = sem("loaded")
        paired = sem("paired")
        high16 = sem("high16")
        low16 = sem("low16")
        multiplied = sem("multiplied")
        cur_high_ready = sem("cur_high_ready")
        cur_low_ready = sem("cur_low_ready")
        summed = sem("summed")
        for_dve = sem("for_dve")
        for_act = sem("for_act")
        mac = sem("mac")
        act_prod = sem("act_prod")
        tree = sem("tree")
        left_free = sem("left_free")
        folded = sem("folded")
        z1_step = sem("z1_step")
        z2_turned = sem("z2_turned")
        z2_ready = sem("z2_ready")
        top_product = sem("top_product")
        top_relu = sem("top_relu")
        y_ready = sem("y_ready")
        y_out = sem("y_out")

        block = ctx.enter_context(nc.Block())
        MACS = HG * EACH
        WRITES, LOADS = 2, 1 + STEPS

        def wait(eng, semaphore, value):
            if not isinstance(value, int) or value > 0:
                eng.wait_ge(semaphore, value)

        def block_of(chunk):
            if isinstance(chunk, int):
                return chunk // CPB
            return (chunk >> (CPB.bit_length() - 1)).with_bounds(min_val=0, max_val=BLOCKS - 1)

        def in_block(chunk):
            if isinstance(chunk, int):
                return chunk % CPB
            return (chunk & (CPB - 1)).with_bounds(min_val=0, max_val=CPB - 1)

        def products_before(chunk, step):
            return (chunk - 1) * STEPS + PRODUCT_ORDER.index(step) + 1

        def body_loop(eng, body):
            body(0, True, False)
            with eng.Fori(1, CHUNKS // UNROLL - 1) as turn:
                body(turn * UNROLL, False, False)
            body(CHUNKS - UNROLL, False, True)

        @block.sync
        def _(sp):
            sp.dma_start(ids_sb[:], ids.rearrange("(k p) f -> p k f", p=P)).then_inc(ids_in, 16)
            sp.dma_start(ident[:], identity).then_inc(w0_in, 16)
            sp.dma_start(w0_sb[:], w0_ab).then_inc(w0_in, 16)
            sp.dma_start(w0_t[:], w0_ba).then_inc(w0_in, 16)
            sp.dma_start(w0_half_sb[:], w0_half).then_inc(w0_in, 16)
            sp.dma_start(parity_sb[:], parity).then_inc(w0_in, 16)
            sp.dma_start(w1_sb[:], w1.rearrange("(h m) n -> m h n", h=F)).then_inc(w1_in, 16)
            sp.dma_start(wt1[:], w_top1[0:2 * P, :].rearrange("(k p) n -> p k n", p=P)).then_inc(top_in, 16)
            sp.dma_start(wt1_dense[:], w_top1[2 * P:, :]).then_inc(top_in, 16)
            sp.dma_start(wt2[:], w_top2.rearrange("(k p) n -> p k n", p=P)).then_inc(top_in, 16)
            sp.dma_start(wt3[:], w_top3).then_inc(top_in, 16)
            sp.dma_start(bt1[:], b_top1).then_inc(top_in, 16)
            sp.dma_start(bt2[:], b_top2).then_inc(top_in, 16)
            sp.dma_start(dense_sb[:], dense_t).then_inc(top_in, 16)

            def shift_through_dram(c, u):
                sp.wait_ge(turned_ready, c + 1)
                wait(sp, loaded, (c - 1) * (LOADS * 16))
                to = x0_dram[u]
                for first_field, fields in ((0, F), (F, SHIFTS)):
                    if first_field > 0:
                        wait(sp, paired, (c - 1) * STEPS)
                    sp.dma_start(to[first_field:first_field + fields, :].rearrange("f (d b) -> (f d) b", d=DC),
                                 turned[0:fields * DC, :]).then_inc(written, 16)
                sp.wait_ge(written, (c + 1) * (WRITES * 16))

                def load(dst, first_field, field_step):
                    src = bass.AP(to.tensor, to.offset + first_field * COLS,
                                  [[COLS, F], [field_step * COLS, COPIES], [1, COLS]])
                    sp.dma_start(dst, src).then_inc(loaded, 16)

                load(x4[u][:], 0, 0)
                load(shifts[u][:, 0, :], SHIFTS, 0)
                for step in range(1, STEPS):
                    load(shifts[u][:, step, :], (step - 1) * COPIES, 1)

            shift_through_dram(0, 0)
            shift_through_dram(1, 1)

            def body(first_chunk, first, last):
                for u in range(UNROLL):
                    if not last:
                        shift_through_dram(first_chunk + u + 2, u)

            body_loop(sp, body)
            sp.wait_ge(y_ready, 1)
            sp.dma_start(out.rearrange("b o -> o b"), y_sb[:]).then_inc(y_out, 16)
            sp.wait_ge(y_out, 16)

        @block.gpsimd
        def _(pool):
            pool.wait_ge(ids_in, 16)
            for f in range(F):
                nc.gpsimd.indirect_dma_start(
                    out=rows[:, 0, f, :], out_offset=None, in_=tables[f],
                    in_offset=bass.IndirectOffsetOnAxis(ids_sb[:, 0, f:f + 1], 0)).then_inc(gathered, 16)

            def sum_parts(pair_no, t):
                tile = pair_no * 2 + t % 2
                src, width, at = parts[t // 2 % 2][t % 2], EACH * HG * N2 // 2, 0
                if t % 2 == 0:
                    pool.wait_ge(act_prod, (pair_no + 1) * (2 * EACH))
                    pool.wait_ge(mac, (pair_no + 1) * (2 * MACS))
                for level in range(TREE):
                    if level > 0:
                        pool.wait_ge(tree, tile * TREE + level)
                    if level == TREE - 1:
                        dst = left[t // 2 % TOTALS][:, t % 2, :, :].rearrange("p l n -> p (l n)")
                        pool.wait_ge(left_free, pair_no + 1)
                    else:
                        dst = half[:, at:at + width]
                    nc.gpsimd.tensor_tensor(dst, src[:, 0:width], src[:, width:2 * width],
                                            ALU.add).then_inc(tree, 1)
                    src, at, width = dst, at + width, width // 2

            tiles = CPB * DC
            rows_at = tiles - 2 * DC - 3
            EARLY = F * (tiles - 1 - rows_at) // tiles
            late = {t: [] for t in range(tiles)}
            for f in range(EARLY, F):
                late[(f - EARLY) * (rows_at - 1) // (F - EARLY)].append(f)
            for f in range(EARLY):
                late[rows_at + 1 + f * (tiles - 1 - rows_at) // EARLY].append(f)

            def gather(f):
                nc.gpsimd.indirect_dma_start(
                    out=rows_next[:, f, :], out_offset=None, in_=tables[f],
                    in_offset=bass.IndirectOffsetOnAxis(ids_next[:, f:f + 1], 0)).then_inc(gathered, 16)

            def fetch_ids(k):
                nc.gpsimd.tensor_copy(ids_next[:], ids_sb[:, bass.ds(k, 1), :].rearrange(
                    "p o f -> p (o f)")).then_inc(ids_moved, 1)
                pool.wait_ge(ids_moved, k)

            def block_body(k, next_block, one_after):
                for t in range(tiles):
                    sum_parts(k * (tiles // 2) + t // 2, t)
                    if next_block and t == rows_at:
                        pool.wait_ge(gathered, (k + 2) * (F * 16))
                        nc.gpsimd.tensor_copy(
                            rows[:, bass.ds(k + 1, 1), :, :].rearrange("p o f d -> p (o f d)"),
                            rows_next[:].rearrange("p f d -> p (f d)")).then_inc(rows_ready, 1)
                        if one_after:
                            fetch_ids(k + 2)
                            pool.wait_ge(rows_ready, k + 2)
                    if (next_block and t < rows_at) or (one_after and t > rows_at):
                        for f in late[t]:
                            gather(f)

            pool.wait_ge(gathered, F * 16)
            nc.gpsimd.memset(half[:, 0:1], 0.0).then_inc(rows_ready, 1)
            fetch_ids(1)
            for f in range(EARLY):
                gather(f)
            with pool.Fori(0, BLOCKS - 2) as k:
                block_body(k, True, True)
            block_body(BLOCKS - 2, True, False)
            block_body(BLOCKS - 1, False, False)

        def rows_of(c):
            return rows[:, bass.ds(block_of(c), 1), :, bass.ds(in_block(c) * DC, DC)].rearrange("p o f d -> p (o f) d")

        def act_x0_waits(act, c):
            wait(act, act_prod, (c - 1) * (2 * EACH * CPAIRS))
            wait(act, mac, (c - 1) * (2 * MACS * CPAIRS))

        def act_x0(act, c, u):
            nc.scalar.copy(x0[u][:], rows_of(c)).then_inc(x0_ready, 1)

        def act_turn_waits(act, c):
            act.wait_ge(rows_ready, block_of(c) + 1)
            wait(act, transposed, c)

        def act_turn(act, c):
            nc.scalar.copy(turn_in[:].rearrange("p (f d) -> p f d", d=DC), rows_of(c)).then_inc(turn_ready, 1)

        def act_turned(act, c):
            act.wait_ge(transposed, c + 1)
            wait(act, written, c * (WRITES * 16))
            nc.scalar.copy(turned[:], turn_bank[:, 0:P]).then_inc(turned_ready, 1)

        def act_high16(act, c):
            act.wait_ge(paired, c * STEPS + PAIR_ORDER.index(0) + 1)
            wait(act, multiplied, products_before(c, 0))
            nc.scalar.copy(pair16_hl[:], pair16[:]).then_inc(high16, 1)

        def act_high(act, c, u):
            act.wait_ge(multiplied, (c + 1) * STEPS)
            wait(act, for_dve, (c - 1) * (2 * EACH * CPAIRS))
            nc.scalar.activation(cur_high[u][:], cur_bank[:], ACT.Relu).then_inc(cur_high_ready, 1)

        @block.scalar
        def _(act):
            act.wait_ge(w0_in, 5 * 16)
            nc.scalar.copy(w0_half_r[:], w0_half_sb[:]).then_inc(w0_half_high, 1)
            act.wait_ge(w1_in, 16)
            nc.scalar.copy(w1_high[:], w1_sb[:].rearrange("m h n -> m (h n)")).then_inc(w1_high_done, 1)
            act_turn_waits(act, 0)
            act_turn(act, 0)
            act_turned(act, 0)
            act_turn_waits(act, 1)
            act_turn(act, 1)
            act_turned(act, 1)
            act_x0(act, 0, 0)
            act_high16(act, 0)
            act_high(act, 0, 0)

            def body(first_chunk, first, last):
                for u in range(UNROLL):
                    c = first_chunk + u
                    for q in range(CPAIRS):
                        pair_no = c * CPAIRS + q
                        if q == 0:
                            act.wait_ge(x0_ready, c + 1)
                        wait(act, tree, (pair_no - 2) * (2 * TREE) + TREE + 1)
                        for e in range(EACH):
                            for ab in range(2):
                                slot = q * 2 * GROUPS + 4 * e + ab
                                if slot == ACT_X0 and not (last and u == UNROLL - 1):
                                    act_x0_waits(act, c + 1)
                                if slot == ACT_TURN and not last:
                                    act_turn_waits(act, c + 2)
                                act.wait_ge(for_act, (pair_no * EACH + e) * 2 + ab + 1)
                                for i in range(HG):
                                    h, at = 2 * e * HG + i, (e * HG + i) * N2
                                    ins = nc.scalar.activation(
                                        parts[q][ab][:, at:at + N2], act_bank[ab][:, i * N2:(i + 1) * N2],
                                        ACT.Copy, scale=x0[u][:, h, 2 * q + ab:2 * q + ab + 1])
                                ins.then_inc(act_prod, 1)
                                if slot == ACT_X0 and not (last and u == UNROLL - 1):
                                    act_x0(act, c + 1, 1 - u)
                                if slot == ACT_HIGH16 and not (last and u == UNROLL - 1):
                                    act_high16(act, c + 1)
                                if slot == ACT_HIGH and not (last and u == UNROLL - 1):
                                    act_high(act, c + 1, 1 - u)
                                if slot == ACT_TURN and not last:
                                    act_turn(act, c + 2)
                                if slot == ACT_TURNED and not last:
                                    act_turned(act, c + 2)

            body_loop(act, body)

            act.wait_ge(z2_turned, 1)
            nc.scalar.copy(z2[:], bank[0][:]).then_inc(z2_ready, 1)
            act.wait_ge(top_in, 7 * 16)
            for i in range(H1 // P):
                act.wait_ge(top_product, i + 1)
                nc.scalar.activation(a1[:, i, :], bank[1 + i][:], ACT.Relu,
                                     bias=bt1[:, i:i + 1]).then_inc(top_relu, 1)
            for i in range(H2 // P):
                act.wait_ge(top_product, H1 // P + i + 1)
                nc.scalar.activation(a2[:, i, :], bank[5 + i][:], ACT.Relu,
                                     bias=bt2[:, i:i + 1]).then_inc(top_relu, 1)
            act.wait_ge(top_product, H1 // P + H2 // P + 1)
            nc.scalar.copy(y_sb[:], bank[7][0:1, :]).then_inc(y_ready, 1)

        def dve_pair(dve, c, u, step):
            dve.wait_ge(loaded, (c + 1) * (LOADS * 16))
            if step == 0:
                wait(dve, low16, c)
                wait(dve, high16, c)
                dst = pair16
            else:
                before = products_before(c + 1, 1) if step == 4 else products_before(c, {1: 4}.get(step, step))
                wait(dve, multiplied, before)
                dst = pair[step % 3]
            nc.vector.tensor_tensor(dst[:], shifts[u][:, step, :], x4[u][:], ALU.mult).then_inc(paired, 1)

        def dve_low16(dve, c):
            dve.wait_ge(high16, c + 1)
            nc.vector.tensor_tensor(pair16_hl[P // 2:, :], pair16[P // 2:, :], pair16_hl[P // 2:, :].bitcast(FP32),
                                    ALU.subtract).then_inc(low16, 1)

        def dve_low(dve, c, u):
            dve.wait_ge(cur_high_ready, c + 1)
            wait(dve, for_dve, (c - 1) * (2 * EACH * CPAIRS))
            nc.vector.scalar_tensor_tensor(
                out=cur_low[u][:], in0=cur_bank[:], scalar=0.0, in1=cur_high[u][:].bitcast(FP32),
                op0=ALU.max, op1=ALU.subtract).then_inc(cur_low_ready, 1)

        def dve_sum(dve, c):
            s1 = sum1[:, bass.ds(block_of(c), 1), :, :].rearrange("p o d b -> p (o d b)")
            wait(dve, summed, c)
            nc.vector.scalar_tensor_tensor(
                out=s1, in0=cur_bank[:], scalar=0.0, in1=s1, op0=ALU.max, op1=ALU.add).then_inc(summed, 1)

        def dve_fold(dve, pair_no, q4, k):
            dve.wait_ge(tree, (pair_no + 1) * (2 * TREE))
            wait(dve, folded, pair_no)
            nc.vector.tensor_tensor(total[:], left[q4][:, :, 0, :], left[q4][:, :, 1, :],
                                    ALU.add).then_inc(left_free, 1)
            dve.wait_ge(left_free, pair_no + TOTALS + 1)
            s2 = sum2[:, bass.ds(k, 1), :, :].rearrange("p o t n -> p (o t n)")
            nc.vector.scalar_tensor_tensor(
                out=s2, in0=total[:].rearrange("p t n -> p (t n)"), scalar=0.0, in1=s2, op0=ALU.max,
                op1=ALU.add).then_inc(folded, 1)

        @block.vector
        def _(dve):
            nc.vector.memset(sum1[:], 0.0).then_inc(zeroed, 1)
            nc.vector.memset(sum2[:], 0.0).then_inc(zeroed, 1)
            nc.vector.memset(total[:], 0.0).then_inc(left_free, TOTALS)
            dve.wait_ge(w0_in, 5 * 16)
            nc.vector.tensor_tensor(w0_sb[:], w0_sb[:], w0_t[:], ALU.add).then_inc(w0_done, 1)
            dve.wait_ge(w0_half_high, 1)
            dve.wait_ge(w0_done, 1)
            nc.vector.tensor_scalar(w0_t[:, 0, :], w0_half_sb[:], parity_sb[:, 0:1], None, ALU.mult).then_inc(w0_done, 1)
            dve.wait_ge(w0_done, 2)
            nc.vector.scalar_tensor_tensor(
                out=w0_half_hl[:], in0=w0_half_r[:].bitcast(FP32), scalar=parity_sb[:, 1:2], in1=w0_t[:, 0, :],
                op0=ALU.mult, op1=ALU.add).then_inc(w0_done, 1)
            dve.wait_ge(w1_high_done, 1)
            nc.vector.tensor_tensor(w1_low[:], w1_sb[:].rearrange("m h n -> m (h n)"), w1_high[:].bitcast(FP32),
                                    ALU.subtract).then_inc(w1_low_done, 1)
            dve.wait_ge(zeroed, 2)
            for step in PAIR_ORDER:
                dve_pair(dve, 0, 0, step)
                if step == PAIR_ORDER[3]:
                    dve_low16(dve, 0)
            dve_low(dve, 0, 0)

            def body(first_chunk, first, last):
                for u in range(UNROLL):
                    c = first_chunk + u
                    for q in range(CPAIRS):
                        pair_no = c * CPAIRS + q
                        for e in range(EACH):
                            slot = q * 2 * GROUPS + 4 * e
                            if slot == DVE_SUM:
                                dve_sum(dve, c)
                            if e == (3, 1)[q] and not (first and u == 0):
                                dve_fold(dve, pair_no - CPAIRS, (u - 1) * CPAIRS % 4 + q, block_of(c - 1))
                            if not (last and u == UNROLL - 1):
                                if slot == DVE_LOW16:
                                    dve_low16(dve, c + 1)
                                if slot in DVE_PAIR:
                                    dve_pair(dve, c + 1, 1 - u, DVE_PAIR[slot])
                                if slot == DVE_LOW:
                                    dve_low(dve, c + 1, 1 - u)
                            dve.wait_ge(for_dve, (pair_no * EACH + e + 1) * 2)
                            for n in range(e * HG, (e + 1) * HG):
                                for ab in range(2):
                                    i, h = n % HG, (2 * e + 1) * HG + n % HG
                                    before = dst = acc[:, u * CPAIRS + q, ab, :]
                                    if n == 0:
                                        before = parts[q][ab][:, 0:N2]
                                        dve.wait_ge(act_prod, pair_no * (2 * EACH) + ab + 1)
                                    else:
                                        dve.wait_ge(mac, pair_no * (2 * MACS) + 2 * n + ab - 1)
                                    if n == MACS - 1:
                                        dst = parts[q][ab][:, 0:N2]
                                    nc.vector.scalar_tensor_tensor(
                                        out=dst, in0=dve_bank[e % 2 * 2 + ab][:, i * N2:(i + 1) * N2],
                                        scalar=x0[u][:, h, 2 * q + ab:2 * q + ab + 1], in1=before, op0=ALU.mult,
                                        op1=ALU.add).then_inc(mac, 1)

            body_loop(dve, body)
            for q in range(CPAIRS):
                dve_fold(dve, (CHUNKS - 1) * CPAIRS + q, CPAIRS + q, BLOCKS - 1)
            dve.wait_ge(folded, CHUNKS * CPAIRS)
            nc.vector.tensor_tensor(z2_rows[:], sum2[:, :, 0, :], sum2[:, :, 1, :], ALU.add).then_inc(z1_step, 1)
            dve.wait_ge(summed, CHUNKS)
            nc.vector.tensor_tensor(z1_half[:], sum1[:, :, 0:2, :], sum1[:, :, 2:4, :], ALU.add).then_inc(z1_step, 1)
            dve.wait_ge(z1_step, 2)
            nc.vector.tensor_tensor(z1[:].rearrange("p (k b) -> p k b", k=BLOCKS), z1_half[:, :, 0, :],
                                    z1_half[:, :, 1, :], ALU.add).then_inc(z1_step, 1)

        def pe_turn(pe, c):
            pe.wait_ge(turn_ready, c + 1)
            wait(pe, turned_ready, c)
            nc.tensor.transpose(turn_bank[:, 0:P], turn_in[:], ident[:]).then_inc(transposed, 1)

        def pe_product(pe, c, step):
            if step == PRODUCT_ORDER[0]:
                wait(pe, summed, c)
            if step == 0:
                pe.wait_ge(low16, c + 1)
                ins = nc.tensor.matmul(cur_bank[:], w0_half_hl[:], pair16_hl[:], start=False, stop=False)
            else:
                pe.wait_ge(paired, c * STEPS + PAIR_ORDER.index(step) + 1)
                ins = nc.tensor.matmul(cur_bank[:], w0_sb[:, step - 1, :], pair[step % 3][:],
                                       start=step == PRODUCT_ORDER[0], stop=step == PRODUCT_ORDER[-1])
            ins.then_inc(multiplied, 1)

        @block.tensor
        def _(pe):
            pe.wait_ge(w0_in, 5 * 16)
            pe_turn(pe, 0)
            pe_turn(pe, 1)
            pe.wait_ge(w0_done, 3)
            for step in PRODUCT_ORDER:
                pe_product(pe, 0, step)
            pe.wait_ge(w1_low_done, 1)

            def body(first_chunk, first, last):
                for u in range(UNROLL):
                    c = first_chunk + u
                    for q in range(CPAIRS):
                        pair_no = c * CPAIRS + q
                        for g in range(GROUPS):
                            e = g // 2
                            for ab in range(2):
                                if g % 2 == 0:
                                    dst, ready = act_bank[ab], for_act
                                    wait(pe, act_prod, (pair_no * EACH + e - 1) * 2 + ab + 1)
                                else:
                                    dst, ready = dve_bank[e % 2 * 2 + ab], for_dve
                                    wait(pe, mac, (pair_no * EACH + e - 1) * (2 * HG))
                                t = 2 * q + ab
                                cols, fields = slice(t * P, (t + 1) * P), slice(g * COLS, (g + 1) * COLS)
                                slot = q * 2 * GROUPS + 2 * g + ab
                                if slot == 0:
                                    pe.wait_ge(cur_high_ready, c + 1)
                                nc.tensor.matmul(dst[:], cur_high[u][:, cols], w1_high[:, fields],
                                                 start=True, stop=False)
                                nc.tensor.matmul(dst[:], cur_high[u][:, cols], w1_low[:, fields],
                                                 start=False, stop=False)
                                if slot == 0:
                                    pe.wait_ge(cur_low_ready, c + 1)
                                nc.tensor.matmul(dst[:], cur_low[u][:, cols], w1_high[:, fields],
                                                 start=False, stop=True).then_inc(ready, 1)
                                if slot in PE_PRODUCT and not (last and u == UNROLL - 1):
                                    pe_product(pe, c + 1, PE_PRODUCT[slot])
                                if slot == PE_TURN and not last:
                                    pe_turn(pe, c + 2)

            body_loop(pe, body)

            pe.wait_ge(z1_step, 1)
            for k in range(BLOCKS):
                last = nc.tensor.transpose(bank[0][:, k * P:(k + 1) * P], z2_rows[:, k, :], ident[:])
            last.then_inc(z2_turned, 1)
            pe.wait_ge(top_in, 7 * 16)
            pe.wait_ge(z1_step, 3)
            pe.wait_ge(act_prod, CHUNKS * DC * EACH)
            for i in range(H1 // P):
                n = slice(i * P, (i + 1) * P)
                nc.tensor.matmul(bank[1 + i][:], wt1[:, 0, n], z1[:], start=True, stop=False)
                nc.tensor.matmul(bank[1 + i][:], wt1_dense[:, n], dense_sb[:], start=False, stop=False)
                if i == 0:
                    pe.wait_ge(z2_ready, 1)
                nc.tensor.matmul(bank[1 + i][:], wt1[:, 1, n], z2[:], start=False, stop=True).then_inc(top_product, 1)
            for i in range(H2 // P):
                for k in range(H1 // P):
                    if i == 0:
                        pe.wait_ge(top_relu, k + 1)
                    ins = nc.tensor.matmul(bank[5 + i][:], wt2[:, k, i * P:(i + 1) * P], a1[:, k, :],
                                           start=k == 0, stop=k == H1 // P - 1)
                ins.then_inc(top_product, 1)
            for k in range(H2 // P):
                pe.wait_ge(top_relu, H1 // P + k + 1)
                ins = nc.tensor.matmul(bank[7][0:1, :], wt3[:, k:k + 1], a2[:, k, :], start=k == 0,
                                       stop=k == H2 // P - 1)
            ins.then_inc(top_product, 1)


def kernel(**inputs):
    import numpy as np
    import concourse.bacc as bacc
    from concourse.bass_utils import run_bass_kernel_spmd

    f0 = np.asarray(inputs["L0_rec_filter_0"]).reshape(F, F, N1)
    h, shift = np.arange(F)[:, None], np.arange(SHIFTS)[None, :]
    partner = (h + shift) % F

    def by_step(w):
        w = w.reshape(F, STEPS - 1, COPIES, N1).transpose(0, 2, 1, 3)
        return np.ascontiguousarray(w.reshape(P, STEPS - 1, N1))

    back = f0[partner, h]
    back[:, 0] = 0
    low_h = np.arange(F) % SHIFTS
    both = np.stack([f0[low_h, low_h + SHIFTS]] * 2 + [f0[low_h + SHIFTS, low_h]] * 2, axis=1)
    odd = np.arange(P) % 2

    arrays = {
        "ids_dram": np.ascontiguousarray(inputs["ids"]),
        "w0_ab_dram": by_step(f0[h, partner]),
        "w0_ba_dram": by_step(back),
        "w0_half_dram": np.ascontiguousarray(both.reshape(P, N1)),
        "parity_dram": np.stack([odd, 1 - 2 * odd], axis=1).astype(np.float32),
        "w1_dram": np.asarray(inputs["L0_rec_filter_1"]).reshape(F * N1, N2),
        "w_top1_dram": np.asarray(inputs["W_top1"]),
        "b_top1_dram": np.ascontiguousarray(np.asarray(inputs["b_top1"]).reshape(H1 // P, P).T),
        "w_top2_dram": np.asarray(inputs["W_top2"]),
        "b_top2_dram": np.ascontiguousarray(np.asarray(inputs["b_top2"]).reshape(H2 // P, P).T),
        "w_top3_dram": np.ascontiguousarray(np.asarray(inputs["W_top3"]).reshape(H2 // P, P).T),
        "dense_dram": np.ascontiguousarray(np.asarray(inputs["dense_ctx"]).T),
        "identity_dram": np.eye(P, dtype=np.float32),
    }
    for f in range(F):
        arrays[f"table_{f}_dram"] = np.asarray(inputs[f"tbl_{f}"])

    nc = bacc.Bacc("TRN2", target_bir_lowering=False, num_devices=1)
    ap = {n: nc.dram_tensor(n, a.shape, mybir.dt.from_np(a.dtype), kind="ExternalInput").ap()
          for n, a in arrays.items()}
    out = nc.dram_tensor("y_dram", (B, 1), FP32, kind="ExternalOutput").ap()
    x0_dram = nc.dram_tensor("x0_scratch", (2, F + SHIFTS, COLS), FP32, kind="Internal").ap()
    dlrm_tower(nc, ap["ids_dram"], [ap[f"table_{f}_dram"] for f in range(F)], ap["w0_ab_dram"], ap["w0_ba_dram"],
               ap["w0_half_dram"], ap["w1_dram"], ap["w_top1_dram"], ap["b_top1_dram"], ap["w_top2_dram"],
               ap["b_top2_dram"], ap["w_top3_dram"], ap["dense_dram"], ap["identity_dram"], ap["parity_dram"],
               x0_dram, out)
    r = run_bass_kernel_spmd(nc, [arrays], core_ids=[0])
    return r.results[0]["y_dram"]
```

```python
from contextlib import ExitStack

import concourse.bass as bass
from concourse import mybir

FP32 = mybir.dt.float32
FP32R = mybir.dt.float32r
INT32 = mybir.dt.int32
ALU = mybir.AluOpType
ACT = mybir.ActivationFunctionType

B, F, D = 512, 32, 32
N1 = N2 = 128
DENSE, H1, H2 = 16, 512, 256
P = 128
BLOCKS = B // P
DC = 4
COLS = DC * P
CPB = D // DC
CHUNKS = BLOCKS * CPB
HG = COLS // N2
GROUPS = F // HG
EACH = GROUPS // 2
SHIFTS = F // 2
COPIES = P // F
UNROLL = 2
CPAIRS = DC // 2
TREE = 3
TOTALS = 4

STEPS = 5
SPLIT = (1, 2)

DVE_PAIR = {0: 1, 4: 0, 8: 2, 12: 3, 16: 4}
PAIR_ORDER = list(DVE_PAIR.values())
ACT_PAIR_HIGH = {5: 1, 13: 2}
ACT_HIGH16, DVE_LOW16 = 9, 12
PE_PRODUCT = {17: 1, 19: 0, 21: 3, 23: 4, 24: 2}
PRODUCT_ORDER = list(PE_PRODUCT.values())
FIRST_ORDER = [1, 2, 3, 4, 0]
ACT_HIGH, DVE_LOW, DVE_SUM = 25, 28, 0
ACT_X0 = 21
ACT_TURN, PE_TURN, ACT_TURNED = 1, 7, 9
DVE_TOTAL, DVE_FOLD = (2, 1), (3, 2)
DVE_Z1_HALF, DVE_Z1, DVE_Z2, PE_Z2, ACT_Z2 = 8, 12, 16, 22, 25

LAST_TABLES = 6
WARM_UP = 16


def dlrm_tower(nc, ids, tables, w0_ab, w0_ba, w0_half, w1, w_top1, b_top1, w_top2, b_top2, w_top3, dense_t,
               identity, parity, select, x0_dram, out):
    ctx = ExitStack()
    with ctx:
        def sb(name, shape, dt=FP32):
            return ctx.enter_context(nc.sbuf_tensor(name, shape, dt))

        def sem(name):
            return ctx.enter_context(nc.semaphore(name))

        ident = sb("ident", [P, P])
        ids_sb = sb("ids_sb", [P, BLOCKS, F], INT32)
        ids_next = sb("ids_next", [P, F], INT32)
        rows_next = sb("rows_next", [P, F, D])
        rows = sb("rows", [P, BLOCKS, F, D])
        x0 = [sb(f"x0_{i}", [P, F, DC]) for i in range(2)]
        turn_in = sb("turn_in", [P, DC * F])
        turned = sb("turned", [P, P])
        x4 = [sb(f"x4_{i}", [P, COLS]) for i in range(2)]
        shifts = [sb(f"shifts_{i}", [P, STEPS, COLS]) for i in range(2)]
        pair = [sb(f"pair_{i}", [P, COLS]) for i in range(STEPS - 1)]
        pair_high = {step: sb(f"pair_high_{step}", [P, COLS], FP32R) for step in SPLIT}
        pair_low = {step: sb(f"pair_low_{step}", [P, COLS], FP32R) for step in SPLIT}
        pair16 = sb("pair16", [P, COLS])
        pair16_hl = sb("pair16_hl", [P, COLS], FP32R)
        w0_sb = sb("w0_sb", [P, STEPS - 1, N1])
        w0_t = sb("w0_t", [P, STEPS - 1, N1])
        w0_high = sb("w0_high", [P, len(SPLIT), N1], FP32R)
        w0_low = sb("w0_low", [P, len(SPLIT), N1], FP32R)
        w0_half_sb = sb("w0_half_sb", [P, N1])
        w0_half_r = sb("w0_half_r", [P, N1], FP32R)
        w0_half_hl = sb("w0_half_hl", [P, N1], FP32R)
        parity_sb = sb("parity_sb", [P, 2])
        w1_sb = sb("w1_sb", [P, F, N2])
        w1_high = sb("w1_high", [P, F * N2], FP32R)
        w1_low = sb("w1_low", [P, F * N2], FP32R)
        cur_high = [sb(f"cur_high_{i}", [P, COLS], FP32R) for i in range(2)]
        cur_low = [sb(f"cur_low_{i}", [P, COLS], FP32R) for i in range(2)]
        sum1 = sb("sum1", [P, BLOCKS, DC, P])
        acc = sb("acc", [P, 4, 2, N2])
        parts = [[sb(f"parts_{i}{j}", [P, EACH * HG * N2]) for j in range(2)] for i in range(2)]
        half = sb("half", [P, 1024 + 512])
        left = [sb(f"left_{i}", [P, 2, 2, N2]) for i in range(TOTALS)]
        total = sb("total", [P, 2, N2])
        sum2 = sb("sum2", [P, BLOCKS, 2, N2])
        wt1 = sb("wt1", [P, 2, H1])
        wt1_dense = sb("wt1_dense", [DENSE, H1])
        wt2 = sb("wt2", [P, H1 // P, H2])
        wt3 = sb("wt3", [P, H2 // P])
        bt1 = sb("bt1", [P, H1 // P])
        bt2 = sb("bt2", [P, H2 // P])
        dense_sb = sb("dense_sb", [DENSE, B])
        z1 = sb("z1", [P, B])
        free = w1_sb[:].rearrange("p h n -> p (h n)")
        a1 = free[:, 0:H1 // P * B].rearrange("p (k b) -> p k b", b=B)
        a2 = free[:, H1 // P * B:(H1 + H2) // P * B].rearrange("p (k b) -> p k b", b=B)
        z1_half = free[:, (H1 + H2) // P * B:][:, 0:BLOCKS * 2 * P].rearrange("p (k h b) -> p k h b", k=BLOCKS, h=2)
        z2, y_sb = pair[1], pair[0][0:1, 0:B]
        z2_rows = rows_next[:].rearrange("p f d -> p (f d)")[:, 0:BLOCKS * N2].rearrange("p (k n) -> p k n", n=N2)
        select_in = parts[0][0][0:F, 0:(1 + STEPS) * P]
        select_sb = [t[0:F, 0:(1 + STEPS) // 2 * P] for t in (cur_high[0], cur_low[0])]
        fields_high, fields_low = cur_high[1][0:F, :], cur_low[1][0:F, :]

        bank = [ctx.enter_context(nc.psum_tensor(f"bank{i}", [P, COLS], FP32)) for i in range(8)]
        dve_bank, cur_bank = bank[0:4], bank[6]

        def act_bank(e, ab):
            return bank[4] if ab == 0 else bank[5 + e % 2 * 2]

        turn_bank = cur_bank
        fields_bank, select_bank = bank[4], [bank[5]] + dve_bank + [bank[4]]
        a1_bank, a2_bank, y_bank = [bank[4], bank[5], bank[7], dve_bank[0]], dve_bank[1:3], dve_bank[3]

        ids_in = sem("ids_in")
        w1_in = sem("w1_in")
        select_read = sem("select_read")
        w0_in = sem("w0_in")
        top_in = sem("top_in")
        zeroed = sem("zeroed")
        w1_high_done = sem("w1_high_done")
        w1_low_done = sem("w1_low_done")
        w0_done = sem("w0_done")
        w0_half_high = sem("w0_half_high")
        w0_high_done = sem("w0_high_done")
        select_ready = sem("select_ready")
        fields_turned = sem("fields_turned")
        fields_split = sem("fields_split")
        selected = sem("selected")
        x4_copied = sem("x4_copied")
        first_gathered = [sem("first_gathered"), sem("last_gathered")]
        gathered = sem("gathered")
        ids_moved = sem("ids_moved")
        rows_ready = sem("rows_ready")
        x0_ready = sem("x0_ready")
        turn_ready = sem("turn_ready")
        transposed = sem("transposed")
        turned_ready = sem("turned_ready")
        written = sem("written")
        loaded = sem("loaded")
        paired = sem("paired")
        pair_high_done = sem("pair_high_done")
        pair_low_done = sem("pair_low_done")
        high16 = sem("high16")
        low16 = sem("low16")
        multiplied = sem("multiplied")
        cur_high_ready = sem("cur_high_ready")
        cur_low_ready = sem("cur_low_ready")
        summed = sem("summed")
        for_dve = sem("for_dve")
        for_act = sem("for_act")
        mac = sem("mac")
        act_prod = sem("act_prod")
        tree = sem("tree")
        left_free = sem("left_free")
        folded = sem("folded")
        last_tree = sem("last_tree")
        z1_step = sem("z1_step")
        z2_step = sem("z2_step")
        z2_turned = sem("z2_turned")
        z2_ready = sem("z2_ready")
        top_product = sem("top_product")
        top_relu = sem("top_relu")
        y_ready = sem("y_ready")
        y_out = sem("y_out")

        block = ctx.enter_context(nc.Block())
        MACS = HG * EACH
        PAIRS = CHUNKS * CPAIRS
        WRITES, LOADS = 2, 1 + STEPS

        def wait(eng, semaphore, value):
            if not isinstance(value, int) or value > 0:
                eng.wait_ge(semaphore, value)

        def block_of(chunk):
            if isinstance(chunk, int):
                return chunk // CPB
            return (chunk >> (CPB.bit_length() - 1)).with_bounds(min_val=0, max_val=BLOCKS - 1)

        def in_block(chunk):
            if isinstance(chunk, int):
                return chunk % CPB
            return (chunk & (CPB - 1)).with_bounds(min_val=0, max_val=CPB - 1)

        def products_before(chunk, step):
            if isinstance(chunk, int) and chunk < 2:
                return (chunk - 1) * STEPS + STEPS
            return (chunk - 1) * STEPS + PRODUCT_ORDER.index(step) + 1

        def body_loop(eng, body):
            body(0, True, False)
            with eng.Fori(1, CHUNKS // UNROLL - 1) as turn:
                body(turn * UNROLL, False, False)
            body(CHUNKS - UNROLL, False, True)

        @block.sync
        def _(sp):
            sp.dma_start(ids_sb[:], ids.rearrange("(k p) f -> p k f", p=P)).then_inc(ids_in, 16)
            sp.dma_start(select_in, select).then_inc(select_read, 16)
            sp.dma_start(ident[:], identity).then_inc(w0_in, 16)
            sp.dma_start(w0_sb[:], w0_ab).then_inc(w0_in, 16)
            sp.dma_start(w0_t[:], w0_ba).then_inc(w0_in, 16)
            sp.dma_start(w0_half_sb[:], w0_half).then_inc(w0_in, 16)
            sp.dma_start(parity_sb[:], parity).then_inc(w0_in, 16)
            sp.dma_start(w1_sb[:], w1.rearrange("(h m) n -> m h n", h=F)).then_inc(w1_in, 16)
            sp.dma_start(wt1[:], w_top1[0:2 * P, :].rearrange("(k p) n -> p k n", p=P)).then_inc(top_in, 16)
            sp.dma_start(wt1_dense[:], w_top1[2 * P:, :]).then_inc(top_in, 16)
            sp.dma_start(wt2[:], w_top2.rearrange("(k p) n -> p k n", p=P)).then_inc(top_in, 16)
            sp.dma_start(wt3[:], w_top3).then_inc(top_in, 16)
            sp.dma_start(bt1[:], b_top1).then_inc(top_in, 16)
            sp.dma_start(bt2[:], b_top2).then_inc(top_in, 16)
            sp.dma_start(dense_sb[:], dense_t).then_inc(top_in, 16)

            def shift_through_dram(c, u):
                sp.wait_ge(turned_ready, c)
                to = x0_dram[u]
                for first_field, fields in ((0, F), (F, SHIFTS)):
                    if first_field > 0:
                        wait(sp, paired, (c - 1) * STEPS)
                    sp.dma_start(to[first_field:first_field + fields, :].rearrange("f (d b) -> (f d) b", d=DC),
                                 turned[0:fields * DC, :]).then_inc(written, 16)
                sp.wait_ge(written, c * (WRITES * 16))

                def load(dst, first_field, field_step):
                    src = bass.AP(to.tensor, to.offset + first_field * COLS,
                                  [[COLS, F], [field_step * COLS, COPIES], [1, COLS]])
                    sp.dma_start(dst, src).then_inc(loaded, 16)

                load(x4[u][:], 0, 0)
                wait(sp, loaded, (c - 1) * (LOADS * 16))
                load(shifts[u][:, 0, :], SHIFTS, 0)
                for step in range(1, STEPS):
                    load(shifts[u][:, step, :], (step - 1) * COPIES, 1)

            shift_through_dram(1, 1)

            def body(first_chunk, first, last):
                for u in range(UNROLL):
                    if not last:
                        shift_through_dram(first_chunk + u + 2, u)

            body_loop(sp, body)
            sp.wait_ge(y_ready, 1)
            sp.dma_start(out.rearrange("b o -> o b"), y_sb).then_inc(y_out, 16)
            sp.wait_ge(y_out, 16)

        @block.gpsimd
        def _(pool):
            pool.wait_ge(ids_in, 16)
            for f in range(F):
                nc.gpsimd.indirect_dma_start(
                    out=rows[:, 0, f, :], out_offset=None, in_=tables[f],
                    in_offset=bass.IndirectOffsetOnAxis(ids_sb[:, 0, f:f + 1], 0)).then_inc(
                        first_gathered[f >= F - LAST_TABLES], 16)

            def sum_parts(pair_no, t):
                tile = pair_no * 2 + t % 2
                src, width, at = parts[t // 2 % 2][t % 2], EACH * HG * N2 // 2, 0
                if t % 2 == 0:
                    pool.wait_ge(act_prod, (pair_no + 1) * (2 * EACH))
                    pool.wait_ge(mac, (pair_no + 1) * (2 * MACS))
                for level in range(TREE):
                    if level > 0:
                        pool.wait_ge(tree, tile * TREE + level)
                    if level == TREE - 1:
                        dst = left[t // 2 % TOTALS][:, t % 2, :, :].rearrange("p l n -> p (l n)")
                        pool.wait_ge(left_free, pair_no + 1)
                    else:
                        dst = half[:, at:at + width]
                    nc.gpsimd.tensor_tensor(dst, src[:, 0:width], src[:, width:2 * width],
                                            ALU.add).then_inc(tree, 1)
                    src, at, width = dst, at + width, width // 2

            def pair_lows(c, which):
                for i in which:
                    step = SPLIT[i]
                    pool.wait_ge(pair_high_done, (c - 1) * len(SPLIT) + i + 1)
                    pool.wait_ge(multiplied, products_before(c, step))
                    nc.gpsimd.tensor_tensor(pair_low[step][:], pair[step - 1][:], pair_high[step][:].bitcast(FP32),
                                            ALU.subtract).then_inc(pair_low_done, 1)

            tiles = CPB * DC
            rows_at = tiles - 2 * DC - 7
            EARLY = F * (tiles - 1 - rows_at) // tiles
            late = {t: [] for t in range(tiles)}
            for f in range(EARLY, F):
                late[(f - EARLY) * (rows_at - 1) // (F - EARLY)].append(f)
            for f in range(EARLY):
                late[rows_at + 1 + f * (tiles - 1 - rows_at) // EARLY].append(f)

            def gather(f):
                nc.gpsimd.indirect_dma_start(
                    out=rows_next[:, f, :], out_offset=None, in_=tables[f],
                    in_offset=bass.IndirectOffsetOnAxis(ids_next[:, f:f + 1], 0)).then_inc(gathered, 16)

            def fetch_ids(k):
                nc.gpsimd.tensor_copy(ids_next[:], ids_sb[:, bass.ds(k, 1), :].rearrange(
                    "p o f -> p (o f)")).then_inc(ids_moved, 1)
                pool.wait_ge(ids_moved, k)

            def block_body(k, next_block, one_after):
                for t in range(tiles if next_block else tiles - 1):
                    if t % DC == DC - 1 and (next_block or t < tiles - DC - 1):
                        pair_lows(k * CPB + t // DC + 2, (0,))
                    if t % DC == 0 and (next_block or t < tiles - DC):
                        pair_lows(k * CPB + t // DC + 1, range(1, len(SPLIT)))
                    sum_parts(k * (tiles // 2) + t // 2, t)
                    if next_block and t == rows_at:
                        pool.wait_ge(gathered, (k + 1) * (F * 16))
                        nc.gpsimd.tensor_copy(
                            rows[:, bass.ds(k + 1, 1), :, :].rearrange("p o f d -> p (o f d)"),
                            rows_next[:].rearrange("p f d -> p (f d)")).then_inc(rows_ready, 1)
                        if one_after:
                            fetch_ids(k + 2)
                            pool.wait_ge(rows_ready, k + 2)
                    if (next_block and t < rows_at) or (one_after and t > rows_at):
                        for f in late[t]:
                            gather(f)

            pool.wait_ge(first_gathered[0], (F - LAST_TABLES) * 16)
            pool.wait_ge(first_gathered[1], LAST_TABLES * 16)
            nc.gpsimd.memset(half[:, 0:1], 0.0).then_inc(rows_ready, 1)
            fetch_ids(1)
            for f in range(EARLY):
                gather(f)
            pair_lows(1, (0,))
            with pool.Fori(0, BLOCKS - 2) as k:
                block_body(k, True, True)
            block_body(BLOCKS - 2, True, False)
            block_body(BLOCKS - 1, False, False)

        def rows_of(c):
            return rows[:, bass.ds(block_of(c), 1), :, bass.ds(in_block(c) * DC, DC)].rearrange("p o f d -> p (o f) d")

        def act_x0_waits(act, c):
            wait(act, act_prod, (c - 1) * (2 * EACH * CPAIRS))
            wait(act, mac, (c - 1) * (2 * MACS * CPAIRS))

        def act_x0(act, c, u):
            nc.scalar.copy(x0[u][:], rows_of(c)).then_inc(x0_ready, 1)

        def act_turn_waits(act, c):
            act.wait_ge(rows_ready, block_of(c) + 1)
            wait(act, transposed, c - 1)

        def act_turn(act, c):
            nc.scalar.copy(turn_in[:].rearrange("p (f d) -> p f d", d=DC), rows_of(c)).then_inc(turn_ready, 1)

        def act_turned(act, c):
            act.wait_ge(transposed, c)
            wait(act, written, (c - 1) * (WRITES * 16))
            nc.scalar.copy(turned[:], turn_bank[:, 0:P]).then_inc(turned_ready, 1)

        def act_pair_high(act, c, step):
            act.wait_ge(paired, c * STEPS + PAIR_ORDER.index(step) + 1)
            wait(act, multiplied, products_before(c, step))
            nc.scalar.copy(pair_high[step][:], pair[step - 1][:]).then_inc(pair_high_done, 1)

        def act_high16(act, c):
            act.wait_ge(paired, c * STEPS + PAIR_ORDER.index(0) + 1)
            wait(act, multiplied, products_before(c, 0))
            nc.scalar.copy(pair16_hl[:], pair16[:]).then_inc(high16, 1)

        def act_high(act, c, u):
            act.wait_ge(multiplied, (c + 1) * STEPS)
            wait(act, for_dve, (c - 1) * (2 * EACH * CPAIRS))
            nc.scalar.activation(cur_high[u][:], cur_bank[:], ACT.Relu).then_inc(cur_high_ready, 1)

        @block.scalar
        def _(act):
            act.wait_ge(select_read, 16)
            for i, dst in enumerate(select_sb):
                width = (1 + STEPS) // 2 * P
                nc.scalar.copy(dst, select_in[:, i * width:(i + 1) * width]).then_inc(select_ready, 1)
            act.wait_ge(w0_in, 5 * 16)
            nc.scalar.copy(w0_half_r[:], w0_half_sb[:]).then_inc(w0_half_high, 1)
            act.wait_ge(w0_done, 1)
            nc.scalar.copy(w0_high[:], w0_sb[:, SPLIT[0] - 1:SPLIT[-1], :]).then_inc(w0_high_done, 1)
            act.wait_ge(w1_in, 16)
            nc.scalar.copy(w1_high[:], w1_sb[:].rearrange("m h n -> m (h n)")).then_inc(w1_high_done, 1)
            act_turn_waits(act, 1)
            act_turn(act, 1)
            act.wait_ge(fields_turned, 1)
            nc.scalar.copy(fields_high, fields_bank[0:F, :]).then_inc(fields_split, 1)
            act_turned(act, 1)
            act.wait_ge(selected, 1)
            nc.scalar.copy(x4[0][:], select_bank[0][:]).then_inc(x4_copied, 1)
            act_x0(act, 0, 0)
            act_high16(act, 0)
            act_high(act, 0, 0)

            def body(first_chunk, first, last):
                for u in range(UNROLL):
                    c = first_chunk + u
                    for q in range(CPAIRS):
                        pair_no = c * CPAIRS + q
                        if q == 0:
                            act.wait_ge(x0_ready, c + 1)
                        for e in range(EACH):
                            for ab in range(2):
                                slot = q * 2 * GROUPS + 4 * e + ab
                                if slot == ACT_X0 and not (last and u == UNROLL - 1):
                                    act_x0_waits(act, c + 1)
                                if slot == ACT_TURN and not last:
                                    act_turn_waits(act, c + 2)
                                if e == 0:
                                    wait(act, tree, (pair_no - 2) * (2 * TREE) + ab * TREE + 1)
                                act.wait_ge(for_act, (pair_no * EACH + e) * 2 + ab + 1)
                                for i in range(HG):
                                    h, at = 2 * e * HG + i, (e * HG + i) * N2
                                    ins = nc.scalar.activation(
                                        parts[q][ab][:, at:at + N2], act_bank(e, ab)[:, i * N2:(i + 1) * N2],
                                        ACT.Copy, scale=x0[u][:, h, 2 * q + ab:2 * q + ab + 1])
                                ins.then_inc(act_prod, 1)
                                if slot == ACT_X0 and not (last and u == UNROLL - 1):
                                    act_x0(act, c + 1, 1 - u)
                                if slot in ACT_PAIR_HIGH and not (last and u == UNROLL - 1):
                                    act_pair_high(act, c + 1, ACT_PAIR_HIGH[slot])
                                if slot == ACT_HIGH16 and not (last and u == UNROLL - 1):
                                    act_high16(act, c + 1)
                                if slot == ACT_HIGH and not (last and u == UNROLL - 1):
                                    act_high(act, c + 1, 1 - u)
                                if slot == ACT_TURN and not last:
                                    act_turn(act, c + 2)
                                if slot == ACT_TURNED and not last:
                                    act_turned(act, c + 2)
                                if slot == ACT_Z2 and last and u == UNROLL - 1:
                                    act.wait_ge(z2_turned, 1)
                                    nc.scalar.copy(z2[:, 0:B - P], turn_bank[:, 0:B - P]).then_inc(z2_ready, 1)

            body_loop(act, body)

            act.wait_ge(z2_turned, 2)
            nc.scalar.copy(z2[:, B - P:], turn_bank[:, B - P:]).then_inc(z2_ready, 1)
            act.wait_ge(top_in, 7 * 16)
            for i in range(H1 // P):
                act.wait_ge(top_product, i + 1)
                nc.scalar.activation(a1[:, i, :], a1_bank[i][:], ACT.Relu,
                                     bias=bt1[:, i:i + 1]).then_inc(top_relu, 1)
            for i in range(H2 // P):
                act.wait_ge(top_product, H1 // P + i + 1)
                nc.scalar.activation(a2[:, i, :], a2_bank[i][:], ACT.Relu,
                                     bias=bt2[:, i:i + 1]).then_inc(top_relu, 1)
            act.wait_ge(top_product, H1 // P + H2 // P + 1)
            nc.scalar.copy(y_sb, y_bank[0:1, :]).then_inc(y_ready, 1)

        def dve_pair(dve, c, u, step):
            shifted = shifts[u][:, step, :]
            if isinstance(c, int) and c == 0:
                i = PAIR_ORDER.index(step) + 1
                dve.wait_ge(selected, 1 + i)
                dve.wait_ge(x4_copied, 1)
                shifted = select_bank[i][:]
            else:
                dve.wait_ge(loaded, c * (LOADS * 16))
            if step == 0:
                wait(dve, low16, c)
                wait(dve, high16, c)
                dst = pair16
            else:
                wait(dve, multiplied, products_before(c, step))
                if step in SPLIT:
                    wait(dve, pair_low_done, (c - 2) * len(SPLIT) + SPLIT.index(step) + 1)
                dst = pair[step - 1]
            nc.vector.tensor_tensor(dst[:], shifted, x4[u][:], ALU.mult).then_inc(paired, 1)

        def dve_low16(dve, c):
            dve.wait_ge(high16, c + 1)
            nc.vector.tensor_tensor(pair16_hl[P // 2:, :], pair16[P // 2:, :], pair16_hl[P // 2:, :].bitcast(FP32),
                                    ALU.subtract).then_inc(low16, 1)

        def dve_low(dve, c, u):
            dve.wait_ge(cur_high_ready, c + 1)
            wait(dve, for_dve, (c - 1) * (2 * EACH * CPAIRS))
            nc.vector.scalar_tensor_tensor(
                out=cur_low[u][:], in0=cur_bank[:], scalar=0.0, in1=cur_high[u][:].bitcast(FP32),
                op0=ALU.max, op1=ALU.subtract).then_inc(cur_low_ready, 1)

        def dve_sum(dve, c):
            s1 = sum1[:, bass.ds(block_of(c), 1), :, :].rearrange("p o d b -> p (o d b)")
            wait(dve, summed, c)
            nc.vector.scalar_tensor_tensor(
                out=s1, in0=cur_bank[:], scalar=0.0, in1=s1, op0=ALU.max, op1=ALU.add).then_inc(summed, 1)

        def dve_z2(dve, first_block, end_block):
            dve.wait_ge(folded, end_block * (PAIRS // BLOCKS))
            n = slice(first_block, end_block)
            nc.vector.tensor_tensor(z2_rows[:, n, :], sum2[:, n, 0, :], sum2[:, n, 1, :], ALU.add).then_inc(z2_step, 1)

        def dve_total(dve, pair_no, q4, tree_steps=None):
            dve.wait_ge(tree, (pair_no + 1) * (2 * TREE) if tree_steps is None else tree_steps)
            wait(dve, folded, pair_no)
            nc.vector.tensor_tensor(total[:], left[q4][:, :, 0, :], left[q4][:, :, 1, :],
                                    ALU.add).then_inc(left_free, 1)

        def dve_fold(dve, pair_no, k):
            dve.wait_ge(left_free, pair_no + TOTALS + 1)
            s2 = sum2[:, bass.ds(k, 1), :, :].rearrange("p o t n -> p (o t n)")
            nc.vector.scalar_tensor_tensor(
                out=s2, in0=total[:].rearrange("p t n -> p (t n)"), scalar=0.0, in1=s2, op0=ALU.max,
                op1=ALU.add).then_inc(folded, 1)

        @block.vector
        def _(dve):
            nc.vector.memset(sum1[:], 0.0).then_inc(zeroed, 1)
            nc.vector.memset(sum2[:], 0.0).then_inc(zeroed, 1)
            nc.vector.memset(total[:], 0.0).then_inc(left_free, TOTALS)
            dve.wait_ge(w0_in, 5 * 16)
            nc.vector.tensor_tensor(w0_sb[:], w0_sb[:], w0_t[:], ALU.add).then_inc(w0_done, 1)
            dve.wait_ge(w0_half_high, 1)
            dve.wait_ge(w0_done, 1)
            nc.vector.tensor_scalar(w0_t[:, 0, :], w0_half_sb[:], parity_sb[:, 0:1], None,
                                    ALU.mult).then_inc(w0_done, 1)
            dve.wait_ge(w0_done, 2)
            nc.vector.scalar_tensor_tensor(
                out=w0_half_hl[:], in0=w0_half_r[:].bitcast(FP32), scalar=parity_sb[:, 1:2], in1=w0_t[:, 0, :],
                op0=ALU.mult, op1=ALU.add).then_inc(w0_done, 1)
            dve.wait_ge(w0_high_done, 1)
            nc.vector.tensor_tensor(w0_low[:], w0_sb[:, SPLIT[0] - 1:SPLIT[-1], :], w0_high[:].bitcast(FP32),
                                    ALU.subtract).then_inc(w0_done, 1)
            dve.wait_ge(w1_high_done, 1)
            nc.vector.tensor_tensor(w1_low[:], w1_sb[:].rearrange("m h n -> m (h n)"), w1_high[:].bitcast(FP32),
                                    ALU.subtract).then_inc(w1_low_done, 1)
            dve.wait_ge(zeroed, 2)
            dve.wait_ge(fields_split, 1)
            nc.vector.tensor_tensor(fields_low, fields_bank[0:F, :], fields_high.bitcast(FP32),
                                    ALU.subtract).then_inc(fields_split, 1)
            for step in PAIR_ORDER:
                dve_pair(dve, 0, 0, step)
            dve_low16(dve, 0)
            dve_low(dve, 0, 0)

            def body(first_chunk, first, last):
                for u in range(UNROLL):
                    c = first_chunk + u
                    for q in range(CPAIRS):
                        pair_no = c * CPAIRS + q
                        for e in range(EACH):
                            slot = q * 2 * GROUPS + 4 * e
                            if slot == DVE_SUM:
                                dve_sum(dve, c)
                            if e == DVE_TOTAL[q] and not (first and u == 0):
                                dve_total(dve, pair_no - CPAIRS, (u - 1) * CPAIRS % 4 + q)
                            if e == DVE_FOLD[q] and not (first and u == 0):
                                dve_fold(dve, pair_no - CPAIRS, block_of(c - 1))
                            if not (last and u == UNROLL - 1):
                                if slot == DVE_LOW16:
                                    dve_low16(dve, c + 1)
                                if slot in DVE_PAIR:
                                    dve_pair(dve, c + 1, 1 - u, DVE_PAIR[slot])
                                if slot == DVE_LOW:
                                    dve_low(dve, c + 1, 1 - u)
                            elif slot == DVE_Z1_HALF:
                                dve.wait_ge(summed, CHUNKS)
                                nc.vector.tensor_tensor(z1_half, sum1[:, :, 0:2, :], sum1[:, :, 2:4, :],
                                                        ALU.add).then_inc(z1_step, 1)
                            elif slot == DVE_Z1:
                                dve.wait_ge(z1_step, 1)
                                nc.vector.tensor_tensor(z1[:].rearrange("p (k b) -> p k b", k=BLOCKS),
                                                        z1_half[:, :, 0, :], z1_half[:, :, 1, :],
                                                        ALU.add).then_inc(z1_step, 1)
                            elif slot == DVE_Z2:
                                dve_z2(dve, 0, BLOCKS - 1)
                            dve.wait_ge(for_dve, (pair_no * EACH + e + 1) * 2)
                            for n in range(e * HG, (e + 1) * HG):
                                for ab in range(2):
                                    i, h = n % HG, (2 * e + 1) * HG + n % HG
                                    before = dst = acc[:, u * CPAIRS + q, ab, :]
                                    if n == 0:
                                        before = parts[q][ab][:, 0:N2]
                                        dve.wait_ge(act_prod, pair_no * (2 * EACH) + ab + 1)
                                    else:
                                        dve.wait_ge(mac, pair_no * (2 * MACS) + 2 * n + ab - 1)
                                    if n == MACS - 1:
                                        dst = parts[q][ab][:, 0:N2]
                                    nc.vector.scalar_tensor_tensor(
                                        out=dst, in0=dve_bank[e % 2 * 2 + ab][:, i * N2:(i + 1) * N2],
                                        scalar=x0[u][:, h, 2 * q + ab:2 * q + ab + 1], in1=before, op0=ALU.mult,
                                        op1=ALU.add).then_inc(mac, 1)

            body_loop(dve, body)
            dve.wait_ge(act_prod, PAIRS * (2 * EACH))
            src, width = parts[CPAIRS - 1][1], EACH * HG * N2 // 2
            for level in range(TREE):
                if level == 0:
                    dve.wait_ge(mac, PAIRS * (2 * MACS))
                else:
                    dve.wait_ge(last_tree, level)
                dst = src[:, 0:width]
                if level == TREE - 1:
                    dst = left[(PAIRS - 1) % TOTALS][:, 1, :, :].rearrange("p l n -> p (l n)")
                nc.vector.tensor_tensor(dst, src[:, 0:width], src[:, width:2 * width], ALU.add).then_inc(last_tree, 1)
                width //= 2
                if level == 0:
                    dve_total(dve, PAIRS - 2, (PAIRS - 2) % TOTALS)
                if level == 1:
                    dve_fold(dve, PAIRS - 2, BLOCKS - 1)
            dve.wait_ge(last_tree, TREE)
            dve_total(dve, PAIRS - 1, (PAIRS - 1) % TOTALS, tree_steps=PAIRS * (2 * TREE) - TREE)
            dve_fold(dve, PAIRS - 1, BLOCKS - 1)
            dve_z2(dve, BLOCKS - 1, BLOCKS)

        def pe_turn(pe, c):
            pe.wait_ge(turn_ready, c)
            wait(pe, summed, c - 1)
            nc.tensor.transpose(turn_bank[:, 0:P], turn_in[:], ident[:]).then_inc(transposed, 1)

        def pe_product(pe, c, step, order=PRODUCT_ORDER, turn=True):
            if step == order[0]:
                wait(pe, summed, c)
                if turn:
                    pe.wait_ge(turned_ready, c + 1)
            if step == 0:
                pe.wait_ge(low16, c + 1)
                terms = [(w0_half_hl[:], pair16_hl[:])]
            elif step in SPLIT and not (isinstance(c, int) and c == 0):
                i = SPLIT.index(step)
                pe.wait_ge(pair_low_done, (c - 1) * len(SPLIT) + i + 1)
                terms = [(w0_high[:, i, :], pair_high[step][:]), (w0_low[:, i, :], pair_high[step][:]),
                         (w0_high[:, i, :], pair_low[step][:])]
            else:
                pe.wait_ge(paired, c * STEPS + PAIR_ORDER.index(step) + 1)
                terms = [(w0_sb[:, step - 1, :], pair[step - 1][:])]
            for i, (filters, products) in enumerate(terms):
                ins = nc.tensor.matmul(cur_bank[:], filters, products, start=step == order[0] and i == 0,
                                       stop=step == order[-1] and i == len(terms) - 1)
            ins.then_inc(multiplied, 1)

        def pe_z2(pe, first_block, end_block):
            pe.wait_ge(z2_step, 1 if first_block == 0 else 2)
            for k in range(first_block, end_block):
                ins = nc.tensor.transpose(turn_bank[:, k * P:(k + 1) * P], z2_rows[:, k, :], ident[:])
            ins.then_inc(z2_turned, 1)

        def keep_busy(count):
            for _ in range(count):
                nc.tensor.matmul(dve_bank[1][:], w1_high[:, 0:P], w1_high[:, 0:COLS], start=True, stop=True)

        @block.tensor
        def _(pe):
            pe.wait_ge(w0_in, 5 * 16)
            pe.wait_ge(w0_done, 4)
            pe.wait_ge(w1_low_done, 1)
            pe.wait_ge(first_gathered[0], (F - LAST_TABLES) * 16)
            keep_busy(WARM_UP)
            pe.wait_ge(rows_ready, 1)
            for d in range(DC):
                ins = nc.tensor.transpose(fields_bank[0:F, d * P:(d + 1) * P], rows[:, 0, :, d], ident[:])
            ins.then_inc(fields_turned, 1)
            pe_turn(pe, 1)
            keep_busy(WARM_UP // 2)
            pe.wait_ge(select_ready, 2)
            pe.wait_ge(fields_split, 2)
            for i, step in enumerate([-1] + PAIR_ORDER):
                at = (1 + step) % 3 * P
                pick = select_sb[(1 + step) // 3][:, at:at + P]
                nc.tensor.matmul(select_bank[i][:], pick, fields_high, start=True, stop=False)
                nc.tensor.matmul(select_bank[i][:], pick, fields_low, start=False, stop=True).then_inc(selected, 1)
            for step in FIRST_ORDER:
                pe_product(pe, 0, step, FIRST_ORDER)

            def body(first_chunk, first, last):
                for u in range(UNROLL):
                    c = first_chunk + u
                    for q in range(CPAIRS):
                        pair_no = c * CPAIRS + q
                        for g in range(GROUPS):
                            e = g // 2
                            for ab in range(2):
                                if g % 2 == 0:
                                    dst, ready = act_bank(e, ab), for_act
                                    wait(pe, act_prod, (pair_no * EACH + e - (1, 2)[ab]) * 2 + ab + 1)
                                else:
                                    dst, ready = dve_bank[e % 2 * 2 + ab], for_dve
                                    wait(pe, mac, (pair_no * EACH + e - 1) * (2 * HG))
                                t = 2 * q + ab
                                cols, fields = slice(t * P, (t + 1) * P), slice(g * COLS, (g + 1) * COLS)
                                slot = q * 2 * GROUPS + 2 * g + ab
                                if slot == 0:
                                    pe.wait_ge(cur_high_ready, c + 1)

                                def product(cur_half, w1_half, **flags):
                                    return nc.tensor.matmul(dst[:], cur_half[u][:, cols], w1_half[:, fields], **flags)

                                product(cur_high, w1_high, start=True, stop=False)
                                if slot == 1:
                                    pe.wait_ge(cur_low_ready, c + 1)
                                    nc.tensor.matmul(act_bank(0, 0)[:], cur_low[u][:, 0:P], w1_high[:, fields],
                                                     start=False, stop=True).then_inc(for_act, 1)
                                product(cur_high, w1_low, start=False, stop=False)
                                if slot > 0:
                                    product(cur_low, w1_high, start=False, stop=True).then_inc(ready, 1)
                                if slot in PE_PRODUCT and not (last and u == UNROLL - 1):
                                    pe_product(pe, c + 1, PE_PRODUCT[slot], turn=not last)
                                if slot == PE_TURN and not last:
                                    pe_turn(pe, c + 2)
                                if slot == PE_Z2 and last and u == UNROLL - 1:
                                    pe_z2(pe, 0, BLOCKS - 1)

            body_loop(pe, body)

            pe.wait_ge(top_in, 7 * 16)
            pe.wait_ge(z1_step, 2)
            pe.wait_ge(act_prod, PAIRS * (2 * EACH))
            for i in range(H1 // P):
                n = slice(i * P, (i + 1) * P)
                if i == H1 // P - 1:
                    pe.wait_ge(mac, PAIRS * (2 * MACS) - 2 * HG)
                nc.tensor.matmul(a1_bank[i][:], wt1[:, 0, n], z1[:], start=True, stop=False)
                nc.tensor.matmul(a1_bank[i][:], wt1_dense[:, n], dense_sb[:], start=False, stop=False)
            keep_busy(6)
            pe_z2(pe, BLOCKS - 1, BLOCKS)
            keep_busy(4)
            pe.wait_ge(z2_ready, 2)
            for i in range(H1 // P):
                n = slice(i * P, (i + 1) * P)
                nc.tensor.matmul(a1_bank[i][:], wt1[:, 1, n], z2[:], start=False, stop=True).then_inc(top_product, 1)
            for i in range(H2 // P):
                for k in range(H1 // P):
                    if i == 0:
                        pe.wait_ge(top_relu, k + 1)
                    ins = nc.tensor.matmul(a2_bank[i][:], wt2[:, k, i * P:(i + 1) * P], a1[:, k, :],
                                           start=k == 0, stop=k == H1 // P - 1)
                ins.then_inc(top_product, 1)
            for k in range(H2 // P):
                pe.wait_ge(top_relu, H1 // P + k + 1)
                ins = nc.tensor.matmul(y_bank[0:1, :], wt3[:, k:k + 1], a2[:, k, :], start=k == 0,
                                       stop=k == H2 // P - 1)
            ins.then_inc(top_product, 1)


def kernel(**inputs):
    import numpy as np
    import concourse.bacc as bacc
    from concourse.bass_utils import run_bass_kernel_spmd

    f0 = np.asarray(inputs["L0_rec_filter_0"]).reshape(F, F, N1)
    h, shift = np.arange(F)[:, None], np.arange(SHIFTS)[None, :]
    partner = (h + shift) % F

    def by_step(w):
        w = w.reshape(F, STEPS - 1, COPIES, N1).transpose(0, 2, 1, 3)
        return np.ascontiguousarray(w.reshape(P, STEPS - 1, N1))

    back = f0[partner, h]
    back[:, 0] = 0
    low_h = np.arange(F) % SHIFTS
    both = np.stack([f0[low_h, low_h + SHIFTS]] * 2 + [f0[low_h + SHIFTS, low_h]] * 2, axis=1)
    odd = np.arange(P) % 2

    copy = np.arange(COPIES)[None, :]
    picked = [h + 0 * copy, h + SHIFTS + 0 * copy] + [h + step * COPIES + copy for step in range(STEPS - 1)]
    select = np.arange(F)[:, None] == np.concatenate([p.ravel() % F for p in picked])[None, :]

    arrays = {
        "ids_dram": np.ascontiguousarray(inputs["ids"]),
        "w0_ab_dram": by_step(f0[h, partner]),
        "w0_ba_dram": by_step(back),
        "w0_half_dram": np.ascontiguousarray(both.reshape(P, N1)),
        "select_dram": select.astype(np.float32),
        "parity_dram": np.stack([odd, 1 - 2 * odd], axis=1).astype(np.float32),
        "w1_dram": np.asarray(inputs["L0_rec_filter_1"]).reshape(F * N1, N2),
        "w_top1_dram": np.asarray(inputs["W_top1"]),
        "b_top1_dram": np.ascontiguousarray(np.asarray(inputs["b_top1"]).reshape(H1 // P, P).T),
        "w_top2_dram": np.asarray(inputs["W_top2"]),
        "b_top2_dram": np.ascontiguousarray(np.asarray(inputs["b_top2"]).reshape(H2 // P, P).T),
        "w_top3_dram": np.ascontiguousarray(np.asarray(inputs["W_top3"]).reshape(H2 // P, P).T),
        "dense_dram": np.ascontiguousarray(np.asarray(inputs["dense_ctx"]).T),
        "identity_dram": np.eye(P, dtype=np.float32),
    }
    for f in range(F):
        arrays[f"table_{f}_dram"] = np.asarray(inputs[f"tbl_{f}"])

    nc = bacc.Bacc("TRN2", target_bir_lowering=False, num_devices=1)
    ap = {n: nc.dram_tensor(n, a.shape, mybir.dt.from_np(a.dtype), kind="ExternalInput").ap()
          for n, a in arrays.items()}
    out = nc.dram_tensor("y_dram", (B, 1), FP32, kind="ExternalOutput").ap()
    x0_dram = nc.dram_tensor("x0_scratch", (2, F + SHIFTS, COLS), FP32, kind="Internal").ap()
    dlrm_tower(nc, ap["ids_dram"], [ap[f"table_{f}_dram"] for f in range(F)], ap["w0_ab_dram"], ap["w0_ba_dram"],
               ap["w0_half_dram"], ap["w1_dram"], ap["w_top1_dram"], ap["b_top1_dram"], ap["w_top2_dram"],
               ap["b_top2_dram"], ap["w_top3_dram"], ap["dense_dram"], ap["identity_dram"], ap["parity_dram"],
               ap["select_dram"], x0_dram, out)
    r = run_bass_kernel_spmd(nc, [arrays], core_ids=[0])
    return r.results[0]["y_dram"]
```
